# Optimizing a Trainium2 kernel written in Bass

```python
import numpy as np
import jax
import jax.numpy as jnp

def _softmax(x, axis=-1):
    return jax.nn.softmax(x, axis=axis)

def _gelu(x):
    return jax.nn.gelu(x, approximate=True)

def _silu(x):
    return jax.nn.silu(x)

def _sigmoid(x):
    return jax.nn.sigmoid(x)

def _layernorm(x, axis=-1, eps=1e-05):
    m = jnp.mean(x, axis=axis, keepdims=True)
    v = jnp.var(x, axis=axis, keepdims=True)
    return (x - m) / jnp.sqrt(v + eps)

def _scatter_add(tgt, idx, src, axis=0):
    return tgt.at[idx].add(src)

def _segment_sum(src, seg, n):
    return jax.ops.segment_sum(src, seg, n)
kernel_name = 'mk_vit_tower_cls_d1_tok_img1024_r4_720e75'

def setup_inputs(seed: int=0):
    np.random.seed(seed)
    _w = jnp.asarray

    def _rec_inputs():
        import jax
        import jax.numpy as jnp
        _rk = jax.random.key(seed)
        x = -0.00016672 + 0.999947 * jax.random.normal(jax.random.fold_in(_rk, 1), (32, 3, 96, 96), jnp.float32)
        cls_tok = 0.02 * jax.random.normal(jax.random.fold_in(_rk, 5), (1, 1, 256), jnp.float32)
        return (x, cls_tok)
    x, cls_tok = _rec_inputs()

    def _L0_tok_setup():
        import jax, jax.numpy as jnp
        import numpy as np
        IMAGE_SIZE = 96
        PATCH = 16
        N_EMBD = 256
        C = 3
        N_PATCHES = (IMAGE_SIZE // PATCH) ** 2
        PATCH_DIM = C * PATCH * PATCH
        key = jax.random.key(seed)
        kx, kw, kb, kp = jax.random.split(key, 4)
        B = 64
        x = jax.random.normal(kx, (B, C, IMAGE_SIZE, IMAGE_SIZE), dtype=jnp.float32)
        bound = 1.0 / np.sqrt(PATCH_DIM)
        W = jax.random.uniform(kw, (N_EMBD, PATCH_DIM), minval=-bound, maxval=bound, dtype=jnp.float32)
        b = jax.random.uniform(kb, (N_EMBD,), minval=-bound, maxval=bound, dtype=jnp.float32)
        pos_embd = jax.random.normal(kp, (1, N_PATCHES, N_EMBD), dtype=jnp.float32) * 0.02
        return {'x': x, 'W': W, 'b': b, 'pos_embd': pos_embd}
    _L0_tok_all = _L0_tok_setup()
    _L0_tok_in = {k: v for k, v in _L0_tok_all.items() if k in ('W', 'b', 'pos_embd')}
    del _L0_tok_all

    def _L0_attn_setup():
        import jax, jax.numpy as jnp
        import numpy as np
        B, N, EMBED, HEADS = (1, 512, 256, 16)
        HD = EMBED // HEADS
        BASE = 10000.0
        EPS = 1e-05

        def _rope(t):
            d = t.shape[-1]
            n = t.shape[-2]
            inv_freq = 1.0 / BASE ** (jnp.arange(0, d, 2, dtype=jnp.float32) / d)
            pos = jnp.arange(n, dtype=jnp.float32)
            ang = pos[:, None] * inv_freq[None, :]
            cos = jnp.concatenate([jnp.cos(ang), jnp.cos(ang)], axis=-1)
            sin = jnp.concatenate([jnp.sin(ang), jnp.sin(ang)], axis=-1)
            t1, t2 = (t[..., :d // 2], t[..., d // 2:])
            rot = jnp.concatenate([-t2, t1], axis=-1)
            return t * cos + rot * sin
        key = jax.random.key(seed)
        ks = jax.random.split(key, 7)
        s = EMBED ** (-0.5)
        return {'x': jax.random.normal(ks[0], (B, N, EMBED), dtype=jnp.float32), 'Wq': jax.random.normal(ks[1], (EMBED, EMBED), dtype=jnp.float32) * s, 'Wk': jax.random.normal(ks[2], (EMBED, EMBED), dtype=jnp.float32) * s, 'Wv': jax.random.normal(ks[3], (EMBED, EMBED), dtype=jnp.float32) * s, 'Wo': jax.random.normal(ks[4], (EMBED, EMBED), dtype=jnp.float32) * s, 'Wg1': jax.random.normal(ks[5], (EMBED, HD), dtype=jnp.float32) * s, 'Wg2': jax.random.normal(ks[6], (HD, EMBED), dtype=jnp.float32) * HD ** (-0.5), 'ln_w': jnp.ones((EMBED,), dtype=jnp.float32), 'ln_b': jnp.zeros((EMBED,), dtype=jnp.float32)}
    _L0_attn_all = _L0_attn_setup()
    _L0_attn_in = {k: v for k, v in _L0_attn_all.items() if k in ('Wq', 'Wk', 'Wv', 'Wo', 'Wg1', 'Wg2', 'ln_w', 'ln_b')}
    del _L0_attn_all

    def _L0_ffn_setup():
        import jax, jax.numpy as jnp
        import numpy as np
        HIDDEN = 256
        N_EXPERTS = 32
        MOE_I = 128
        N_GROUP = 4
        TOPK_GROUP = 2
        TOP_K = 6
        N_LOCAL_GROUPS = 16
        ANCHOR_I = 64
        SHARED_I = 128
        ROUTED_SCALE = 0.2
        ANCHOR_ALPHA = 0.1
        BATCH, SEQ = (1, 256)

        def _moe_forward(hidden_states, gate_weight, gate_bias, w_gate, w_up, w_down, shared_w_gate, shared_w_up, shared_w_down, anchor_w_gate, anchor_w_up, anchor_w_down):
            B, S, H = hidden_states.shape
            x = hidden_states.reshape(-1, H)
            T = x.shape[0]
            E = gate_weight.shape[0]
            L = anchor_w_gate.shape[0]
            logits = x @ gate_weight.T
            scores = jax.nn.sigmoid(logits)
            sc = scores + gate_bias
            grp = sc.reshape(T, N_GROUP, E // N_GROUP)
            group_scores = jax.lax.top_k(grp, 2)[0].sum(-1)
            _, gidx = jax.lax.top_k(group_scores, TOPK_GROUP)
            gmask = jax.nn.one_hot(gidx, N_GROUP, dtype=sc.dtype).sum(1)
            emask = jnp.repeat(gmask, E // N_GROUP, axis=1)
            masked = jnp.where(emask > 0, sc, -jnp.inf)
            _, topidx = jax.lax.top_k(masked, TOP_K)
            tw = jnp.take_along_axis(scores, topidx, axis=-1)
            tw = tw / (tw.sum(-1, keepdims=True) + 1e-20) * ROUTED_SCALE
            g = jnp.einsum('th,ehi->tei', x, w_gate)
            u = jnp.einsum('th,ehi->tei', x, w_up)
            eo = jnp.einsum('tei,eih->teh', jax.nn.silu(g) * u, w_down)
            cw = (jax.nn.one_hot(topidx, E, dtype=x.dtype) * tw[..., None]).sum(1)
            routed = jnp.einsum('te,teh->th', cw, eo)
            shared = jax.nn.silu(x @ shared_w_gate) * (x @ shared_w_up) @ shared_w_down
            lg = topidx[:, 0] // (E // L)
            ag = jnp.einsum('th,lhi->tli', x, anchor_w_gate)
            au = jnp.einsum('th,lhi->tli', x, anchor_w_up)
            ao = jnp.einsum('tli,lih->tlh', jax.nn.silu(ag) * au, anchor_w_down)
            acw = jax.nn.one_hot(lg, L, dtype=x.dtype)
            anchor = jnp.einsum('tl,tlh->th', acw, ao)
            out = routed + shared + ANCHOR_ALPHA * anchor
            return out.reshape(B, S, H)
        key = jax.random.key(seed)
        ks = jax.random.split(key, 13)
        s = 0.02
        return {'hidden_states': jax.random.normal(ks[0], (BATCH, SEQ, HIDDEN), jnp.float32), 'gate_weight': s * jax.random.normal(ks[1], (N_EXPERTS, HIDDEN), jnp.float32), 'gate_bias': s * jax.random.normal(ks[2], (N_EXPERTS,), jnp.float32), 'w_gate': s * jax.random.normal(ks[3], (N_EXPERTS, HIDDEN, MOE_I), jnp.float32), 'w_up': s * jax.random.normal(ks[4], (N_EXPERTS, HIDDEN, MOE_I), jnp.float32), 'w_down': s * jax.random.normal(ks[5], (N_EXPERTS, MOE_I, HIDDEN), jnp.float32), 'shared_w_gate': s * jax.random.normal(ks[6], (HIDDEN, SHARED_I), jnp.float32), 'shared_w_up': s * jax.random.normal(ks[7], (HIDDEN, SHARED_I), jnp.float32), 'shared_w_down': s * jax.random.normal(ks[8], (SHARED_I, HIDDEN), jnp.float32), 'anchor_w_gate': s * jax.random.normal(ks[9], (N_LOCAL_GROUPS, HIDDEN, ANCHOR_I), jnp.float32), 'anchor_w_up': s * jax.random.normal(ks[10], (N_LOCAL_GROUPS, HIDDEN, ANCHOR_I), jnp.float32), 'anchor_w_down': s * jax.random.normal(ks[11], (N_LOCAL_GROUPS, ANCHOR_I, HIDDEN), jnp.float32)}
    _L0_ffn_all = _L0_ffn_setup()
    _L0_ffn_in = {k: v for k, v in _L0_ffn_all.items() if k in ('gate_weight', 'gate_bias', 'w_gate', 'w_up', 'w_down', 'shared_w_gate', 'shared_w_up', 'shared_w_down', 'anchor_w_gate', 'anchor_w_up', 'anchor_w_down')}
    del _L0_ffn_all
    return {'x': x, 'cls_tok': cls_tok, 'L0_tok_W': _L0_tok_in['W'], 'L0_tok_b': _L0_tok_in['b'], 'L0_tok_pos_embd': _L0_tok_in['pos_embd'], 'L0_attn_Wq': _L0_attn_in['Wq'], 'L0_attn_Wk': _L0_attn_in['Wk'], 'L0_attn_Wv': _L0_attn_in['Wv'], 'L0_attn_Wo': _L0_attn_in['Wo'], 'L0_attn_Wg1': _L0_attn_in['Wg1'], 'L0_attn_Wg2': _L0_attn_in['Wg2'], 'L0_attn_ln_w': _L0_attn_in['ln_w'], 'L0_attn_ln_b': _L0_attn_in['ln_b'], 'L0_ffn_gate_weight': _L0_ffn_in['gate_weight'], 'L0_ffn_gate_bias': _L0_ffn_in['gate_bias'], 'L0_ffn_w_gate': _L0_ffn_in['w_gate'], 'L0_ffn_w_up': _L0_ffn_in['w_up'], 'L0_ffn_w_down': _L0_ffn_in['w_down'], 'L0_ffn_shared_w_gate': _L0_ffn_in['shared_w_gate'], 'L0_ffn_shared_w_up': _L0_ffn_in['shared_w_up'], 'L0_ffn_shared_w_down': _L0_ffn_in['shared_w_down'], 'L0_ffn_anchor_w_gate': _L0_ffn_in['anchor_w_gate'], 'L0_ffn_anchor_w_up': _L0_ffn_in['anchor_w_up'], 'L0_ffn_anchor_w_down': _L0_ffn_in['anchor_w_down']}

def reference(x, cls_tok, L0_tok_W, L0_tok_b, L0_tok_pos_embd, L0_attn_Wq, L0_attn_Wk, L0_attn_Wv, L0_attn_Wo, L0_attn_Wg1, L0_attn_Wg2, L0_attn_ln_w, L0_attn_ln_b, L0_ffn_gate_weight, L0_ffn_gate_bias, L0_ffn_w_gate, L0_ffn_w_up, L0_ffn_w_down, L0_ffn_shared_w_gate, L0_ffn_shared_w_up, L0_ffn_shared_w_down, L0_ffn_anchor_w_gate, L0_ffn_anchor_w_up, L0_ffn_anchor_w_down):
    import jax
    import jax.numpy as jnp

    def _L0_tok_ref(x, W, b, pos_embd):
        import jax, jax.numpy as jnp
        import numpy as np
        IMAGE_SIZE = 96
        PATCH = 16
        N_EMBD = 256
        C = 3
        N_PATCHES = (IMAGE_SIZE // PATCH) ** 2
        PATCH_DIM = C * PATCH * PATCH
        B, Cc, H, Wd = x.shape
        p = PATCH
        Hp, Wp = (H // p, Wd // p)
        patches = x.reshape(B, Cc, Hp, p, Wp, p)
        patches = patches.transpose(0, 2, 4, 1, 3, 5)
        patches = patches.reshape(B, Hp * Wp, Cc * p * p)
        out = jnp.einsum('bnd,ed->bne', patches, W) + b + pos_embd
        return out

    def _L0_attn_ref(x, Wq, Wk, Wv, Wo, Wg1, Wg2, ln_w, ln_b):
        import jax, jax.numpy as jnp
        import numpy as np
        B, N, EMBED, HEADS = (1, 512, 256, 16)
        HD = EMBED // HEADS
        BASE = 10000.0
        EPS = 1e-05

        def _rope(t):
            d = t.shape[-1]
            n = t.shape[-2]
            inv_freq = 1.0 / BASE ** (jnp.arange(0, d, 2, dtype=jnp.float32) / d)
            pos = jnp.arange(n, dtype=jnp.float32)
            ang = pos[:, None] * inv_freq[None, :]
            cos = jnp.concatenate([jnp.cos(ang), jnp.cos(ang)], axis=-1)
            sin = jnp.concatenate([jnp.sin(ang), jnp.sin(ang)], axis=-1)
            t1, t2 = (t[..., :d // 2], t[..., d // 2:])
            rot = jnp.concatenate([-t2, t1], axis=-1)
            return t * cos + rot * sin
        b, n, _ = x.shape
        q = jax.nn.silu(x @ Wq)
        k = jax.nn.silu(x @ Wk)
        v = x @ Wv
        split = lambda t: t.reshape(b, n, HEADS, HD).transpose(0, 2, 1, 3)
        q, k, v = (split(q), split(k), split(v))
        q = _rope(q)
        k = _rope(k)
        energy = jnp.einsum('bhnd,bhmd->bhnm', q, k)
        mask = jnp.tril(jnp.ones((n, n), dtype=energy.dtype))
        energy = energy * mask
        out = jnp.einsum('bhnm,bhmd->bhnd', energy, v)
        out = out.transpose(0, 2, 1, 3).reshape(b, n, EMBED)
        gate = jax.nn.sigmoid(x @ Wg1 @ Wg2)
        out = out * gate
        mu = out.mean(axis=-1, keepdims=True)
        var = ((out - mu) ** 2).mean(axis=-1, keepdims=True)
        out = (out - mu) / jnp.sqrt(var + EPS) * ln_w + ln_b
        return out @ Wo

    def _L0_ffn_ref(hidden_states, gate_weight, gate_bias, w_gate, w_up, w_down, shared_w_gate, shared_w_up, shared_w_down, anchor_w_gate, anchor_w_up, anchor_w_down):
        import jax, jax.numpy as jnp
        import numpy as np
        HIDDEN = 256
        N_EXPERTS = 32
        MOE_I = 128
        N_GROUP = 4
        TOPK_GROUP = 2
        TOP_K = 6
        N_LOCAL_GROUPS = 16
        ANCHOR_I = 64
        SHARED_I = 128
        ROUTED_SCALE = 0.2
        ANCHOR_ALPHA = 0.1
        BATCH, SEQ = (1, 256)

        def _moe_forward(hidden_states, gate_weight, gate_bias, w_gate, w_up, w_down, shared_w_gate, shared_w_up, shared_w_down, anchor_w_gate, anchor_w_up, anchor_w_down):
            B, S, H = hidden_states.shape
            x = hidden_states.reshape(-1, H)
            T = x.shape[0]
            E = gate_weight.shape[0]
            L = anchor_w_gate.shape[0]
            logits = x @ gate_weight.T
            scores = jax.nn.sigmoid(logits)
            sc = scores + gate_bias
            grp = sc.reshape(T, N_GROUP, E // N_GROUP)
            group_scores = jax.lax.top_k(grp, 2)[0].sum(-1)
            _, gidx = jax.lax.top_k(group_scores, TOPK_GROUP)
            gmask = jax.nn.one_hot(gidx, N_GROUP, dtype=sc.dtype).sum(1)
            emask = jnp.repeat(gmask, E // N_GROUP, axis=1)
            masked = jnp.where(emask > 0, sc, -jnp.inf)
            _, topidx = jax.lax.top_k(masked, TOP_K)
            tw = jnp.take_along_axis(scores, topidx, axis=-1)
            tw = tw / (tw.sum(-1, keepdims=True) + 1e-20) * ROUTED_SCALE
            g = jnp.einsum('th,ehi->tei', x, w_gate)
            u = jnp.einsum('th,ehi->tei', x, w_up)
            eo = jnp.einsum('tei,eih->teh', jax.nn.silu(g) * u, w_down)
            cw = (jax.nn.one_hot(topidx, E, dtype=x.dtype) * tw[..., None]).sum(1)
            routed = jnp.einsum('te,teh->th', cw, eo)
            shared = jax.nn.silu(x @ shared_w_gate) * (x @ shared_w_up) @ shared_w_down
            lg = topidx[:, 0] // (E // L)
            ag = jnp.einsum('th,lhi->tli', x, anchor_w_gate)
            au = jnp.einsum('th,lhi->tli', x, anchor_w_up)
            ao = jnp.einsum('tli,lih->tlh', jax.nn.silu(ag) * au, anchor_w_down)
            acw = jax.nn.one_hot(lg, L, dtype=x.dtype)
            anchor = jnp.einsum('tl,tlh->th', acw, ao)
            out = routed + shared + ANCHOR_ALPHA * anchor
            return out.reshape(B, S, H)
        return _moe_forward(hidden_states, gate_weight, gate_bias, w_gate, w_up, w_down, shared_w_gate, shared_w_up, shared_w_down, anchor_w_gate, anchor_w_up, anchor_w_down)
    h = _L0_tok_ref(x, L0_tok_W, L0_tok_b, L0_tok_pos_embd)
    h = jnp.concatenate([jnp.broadcast_to(cls_tok, (h.shape[0], 1, h.shape[2])), h], axis=1)
    h = h + _L0_attn_ref(_layernorm(h, axis=-1), L0_attn_Wq, L0_attn_Wk, L0_attn_Wv, L0_attn_Wo, L0_attn_Wg1, L0_attn_Wg2, L0_attn_ln_w, L0_attn_ln_b)
    h = h + _L0_ffn_ref(_layernorm(h, axis=-1), L0_ffn_gate_weight, L0_ffn_gate_bias, L0_ffn_w_gate, L0_ffn_w_up, L0_ffn_w_down, L0_ffn_shared_w_gate, L0_ffn_shared_w_up, L0_ffn_shared_w_down, L0_ffn_anchor_w_gate, L0_ffn_anchor_w_up, L0_ffn_anchor_w_down)
    return h

_drawn_inputs = setup_inputs


def setup_inputs(seed=0):
    import zlib

    import numpy as np

    out = dict(_drawn_inputs(seed))
    spreads = {'L0_attn_ln_w': (1.0, 0.2), 'L0_attn_ln_b': (0.0, 0.1)}
    factors = {'L0_ffn_gate_weight': 8.0,
     'L0_ffn_gate_bias': 8.0,
     'L0_ffn_w_gate': 8.0,
     'L0_ffn_w_up': 8.0,
     'L0_ffn_w_down': 8.0,
     'L0_ffn_shared_w_gate': 5.806,
     'L0_ffn_shared_w_up': 5.765,
     'L0_ffn_shared_w_down': 5.711,
     'L0_ffn_anchor_w_gate': 8.0,
     'L0_ffn_anchor_w_up': 8.0,
     'L0_ffn_anchor_w_down': 8.0}
    for name, (base, spread) in spreads.items():
        noise = np.random.default_rng([zlib.crc32(name.encode()), seed]).standard_normal(out[name].shape)
        drawn = base * np.exp(spread * noise) if base else spread * noise
        out[name] = jnp.asarray(drawn.astype(out[name].dtype))
    for name, factor in factors.items():
        out[name] = (out[name] * factor).astype(out[name].dtype)
    return out
```

```python
from contextlib import ExitStack

import numpy as np

import concourse.bass as bass
from concourse import mybir

F32 = mybir.dt.float32
I32 = mybir.dt.int32
U32 = mybir.dt.uint32
ALU = mybir.AluOpType
ACT = mybir.ActivationFunctionType
AX = mybir.AxisListType

P = 128
D = 256
KC = D // P
IMAGES, PATCHES = 32, 36
SEQ = PATCHES + 1
TOKENS = IMAGES * SEQ
PC = 3 * 16 * 16 // P
HEADS, HD = 16, 16
TT = 3 * SEQ
TILES = [TT] * (IMAGES // 3) + [IMAGES % 3 * SEQ]
NT = len(TILES)
BLOCKS = [[0, 1, 2, 3], [4, 5, 6, 7], [8, 9, 10]]
BT = 4 * TT
EPS = 1e-5
EXPERTS, GROUPS, TOPK = 32, 4, 6
GE = EXPERTS // GROUPS
ANCHORS = 16
LISTS = EXPERTS + ANCHORS
CHOICES = TOPK + 1
ROUTED_SCALE, ANCHOR_ALPHA = 0.2, 0.1
WX = 3 * D
LIST_ROWS = TOKENS + P
DUMMY_ROW = LISTS * LIST_ROWS
ROW = D + LISTS + 1
ROUTED_TILES = (TOKENS * TOPK + EXPERTS * (P - 1)) // P
ANCHOR_TILES = (TOKENS + ANCHORS * (P - 1)) // P
XT = ROUTED_TILES + ANCHOR_TILES
CH = 4
OUT_ROWS = 11 * P
LATE = 20
BIG = 3.0e38
assert XT % CH == 0


def cols(t):
    return (t % 4) * TT


def build(nc, pt, wt, posr, brow, wqkv, wo, wg1, wg2, lnwb, gwt, gbias, sgu, sd, wx,
          ident_c, cmask_c, hmask_c, cs_c, before_c, small_c, out):
    with ExitStack() as ctx:
        def sb(name, shape, dt=F32):
            return ctx.enter_context(nc.sbuf_tensor(name, shape, dt))

        def sem(name):
            return ctx.enter_context(nc.semaphore(name))

        W = sb("W", [P, LISTS * WX])
        taken = [LATE * WX]

        def early(shape):
            n = int(np.prod(shape))
            v = W[:, taken[0]:taken[0] + n]
            taken[0] += n
            assert taken[0] <= LISTS * WX
            if len(shape) == 2:
                return v.rearrange("p (a b) -> p a b", b=shape[1])
            if len(shape) == 3:
                return v.rearrange("p (a b c) -> p a b c", b=shape[1], c=shape[2])
            return v

        patches = early([2, PC, BT])
        w_patch = early([PC, D])
        qk = early([4, 2 * D])
        v_sb = early([4, D])
        q_heads = early([2, HEADS, TT])
        gate_th = early([4, D])

        w_qkv = early([KC, 3 * D])
        w_o = early([KC, D])
        w_g1 = sb("w_g1", [P, KC, HD])
        w_g2 = early([D])[0:HD]
        ln_wb = sb("ln_wb", [P, KC, 2])
        w_route = sb("w_route", [P, KC, EXPERTS])
        bias_rt = sb("bias_rt", [P, EXPERTS])
        w_sgu = sb("w_sgu", [P, KC, D])
        w_sd = sb("w_sd", [P, D])
        ident = sb("ident", [P, P])
        causal = sb("causal", [TT, TT])
        hmask = sb("hmask", [P, HEADS // KC])
        cossin = sb("cossin", [TT, 2, HD])
        before = sb("before", [P, P])
        ones = sb("ones", [P, P])
        small = sb("small", [P, 2 * LISTS + 16 + 2])
        iota_l, base0, tri4, pcol = (small[:, 0:LISTS], small[:, LISTS:2 * LISTS],
                                     small[:, 2 * LISTS:2 * LISTS + 16], small[:, 2 * LISTS + 16:2 * LISTS + 17])
        posb = early([D])[0:TT]
        brow_sb = early([D])[0:TT]
        h = sb("h", [P, NT, D])
        xrow = sb("xrow", [P, NT, ROW])
        xrow_i = xrow[:, :, :].bitcast(I32)
        x2T = sb("x2T", [P, KC, TOKENS])
        xn = early([4, D])
        xnT = early([KC, BT])
        rp = early([2, 2 * D])
        g1T = sb("g1T", [HD, 2, TT])
        kT = early([2, KC, TT])
        ynT = early([2, KC, TT])
        e_sb = sb("e_sb", [P, 2 * HEADS * TT])
        energy = e_sb[:, :].rearrange("p (u h t) -> p u h t", u=2, h=HEADS)
        stats = sb("stats", [P, 4, 6])
        mv = sb("mv", [P, 4, 2])
        nwt = sb("nwt", [P, 3, 4])
        nwt_i = nwt[:, :, :].bitcast(I32)
        sig = sb("sig", [P, 2, EXPERTS])
        sc = sb("sc", [P, EXPERTS])
        top8 = sb("top8", [P, GROUPS, 8])
        gs = sb("gs", [P, 4, GROUPS])
        cmp = sb("cmp", [P, 2, GROUPS, GROUPS])
        tv = sb("tv", [P, 8])
        ti = sb("ti", [P, 8], U32)
        ai = sb("ai", [P, 1], U32)
        idx = sb("idx", [P, CHOICES])
        oh = sb("oh", [P, 2, CHOICES, LISTS])
        prod = early([CHOICES, LISTS])
        chosen = sb("chosen", [P, 2, LISTS])
        base = sb("base", [P, LISTS])
        rnk = sb("rnk", [P, LISTS])
        slot_f = sb("slot_f", [P, CHOICES])
        slot = sb("slot", [P, NT, CHOICES], I32)
        wsum = sb("wsum", [P, 2])
        cnt_i = sb("cnt_i", [P, LISTS], I32)
        tabf = sb("tabf", [P, 6, LISTS])
        tcol = sb("tcol", [P, 4])
        table = sb("table", [1, 2, P], I32)
        pad_at = sb("pad_at", [1, LISTS], I32)
        padrow = sb("padrow", [P, ROW])
        padrow_i = padrow[:, :].bitcast(I32)
        at = [0]

        def later(n):
            v = e_sb[:, at[0]:at[0] + n]
            at[0] += n
            assert at[0] <= 2 * HEADS * TT
            return v

        G = later(4 * ROW).rearrange("p (u r) -> p u r", u=4)
        GT = later(2 * D).rearrange("p (u k s) -> p u k s", u=2, k=KC)
        S = later(2 * P).rearrange("p (u s) -> p u s", u=2)
        H = later(2 * P).rearrange("p (u s) -> p u s", u=2)
        HT = later(2 * P).rearrange("p (u s) -> p u s", u=2)
        Y = later(4 * D).rearrange("p (u s) -> p u s", u=4)
        G_i = G.bitcast(I32)
        wcol = sb("wcol", [P, XT])
        tok_of = sb("tok_of", [P, XT], I32)
        tok = sb("tok", [P, CH], I32)
        acc = W[:, 0:2 * CH * D].rearrange("p (u c d) -> p u c d", u=2, c=CH)

        B = [ctx.enter_context(nc.psum_tensor(f"B{i}", [P, 512], F32)) for i in range(8)]

        rows_d = nc.dram_tensor("rows_d", [DUMMY_ROW + P, ROW], F32).ap()
        sums_d = [nc.dram_tensor(f"sums{c}_d", [OUT_ROWS, D], F32).ap() for c in range(CH)]

        ld = {n: sem(f"ld_{n}") for n in ("patch0", "patch1", "patch2", "first", "consts", "rest", "lists", "late")}
        posb_ok, h_emb, xn_ok, xnT_ok = sem("posb_ok"), sem("h_emb"), sem("xn_ok"), sem("xnT_ok")
        emb_ps, xnT_ps, qk_ps, v_ps = sem("emb_ps"), sem("xnT_ps"), sem("qk_ps"), sem("v_ps")
        qk_ok, v_ok, g1_ps, g1_ok = sem("qk_ok"), sem("v_ok"), sem("g1_ps"), sem("g1_ok")
        gate_ps, gate_ok, rope_ok = sem("gate_ps"), sem("gate_ok"), sem("rope_ok")
        qkT_ps, qh_ok, kT_ok = sem("qkT_ps"), sem("qh_ok"), sem("kT_ok")
        en_ps, en_ok, av_ps, og_ok = sem("en_ps"), sem("en_ok"), sem("av_ps"), sem("og_ok")
        yn_ok, ynT_ps, ynT_ok, wo_ps, h2_ok = sem("yn_ok"), sem("ynT_ps"), sem("ynT_ok"), sem("wo_ps"), sem("h2_ok")
        x2_ok, x2T_ps, x2T_ok = sem("x2_ok"), sem("x2T_ps"), sem("x2T_ok")
        rt_ps, rt_ok, ch_ok, rank_ps, slot_ok = (sem("rt_ps"), sem("rt_ok"), sem("ch_ok"), sem("rank_ps"), sem("slot_ok"))
        dchain = sem("dchain")
        ini, ini_d = sem("ini"), sem("ini_d")
        scat, pads = sem("scat"), sem("pads")
        cols_ok, table_ps, table_ok, pad_ok = sem("cols_ok"), sem("table_ps"), sem("table_ok"), sem("pad_ok")
        sgu_ps, ssilu_ok, sh_ok, shT_ps, shT_ok, sd_ps, hs_ok = (
            sem("sgu_ps"), sem("ssilu_ok"), sem("sh_ok"), sem("shT_ps"), sem("shT_ok"), sem("sd_ps"), sem("hs_ok"))
        g_ld = [sem(f"g_ld{u}") for u in range(4)]
        T_ps, gt_ok, U_ps, silu_ok, H_ok, HT_ps, HT_ok, D_ps, Y_ok = (
            sem("T_ps"), sem("gt_ok"), sem("U_ps"), sem("silu_ok"), sem("H_ok"), sem("HT_ps"), sem("HT_ok"),
            sem("D_ps"), sem("Y_ok"))
        added = [sem(f"added{c}") for c in range(CH)]
        meta_ok, tok_ok = sem("meta_ok"), sem("tok_ok")
        fin_ld = [sem("fin_ld0"), sem("fin_ld1")]
        fin_ok, out_st = sem("fin_ok"), sem("out_st")
        block = ctx.enter_context(nc.Block())

        def group_wait(eng, s, n):
            if n > 0:
                eng.wait_ge(s, n)

        def groups(eng, body, n, lag=0):
            for i in range(4):
                body(i)
            with eng.Fori(1, n // 4 - 1) as j:
                for u in range(4):
                    body(4 * j + u, u)
            for i in range(n - 4, n):
                body(i)

        @block.sync
        def _(sp):
            def load_patches(b):
                n = sum(TILES[t] for t in BLOCKS[b])
                sp.dma_start(patches[:, b % 2, :, 0:n], pt[:, :, b * BT:b * BT + n]).then_inc(ld[f"patch{b}"], 16)

            sp.dma_start(w_patch, wt).then_inc(ld["first"], 16)
            load_patches(0)
            for dst, src in ((posb, posr), (brow_sb, brow)):
                sp.dma_start(dst[:, :], src).then_inc(ld["first"], 16)
            for dst, src in ((ident, ident_c), (small, small_c)):
                sp.dma_start(dst[:, :], src).then_inc(ld["consts"], 16)
            sp.dma_start(w_qkv[:, :, :], wqkv).then_inc(ld["consts"], 16)
            sp.dma_start(cossin[:, :, :], cs_c).then_inc(ld["consts"], 16)
            for dst, src in ((causal, cmask_c), (hmask, hmask_c), (before, before_c), (w_g2, wg2), (bias_rt, gbias),
                             (w_sd, sd)):
                sp.dma_start(dst[:, :], src).then_inc(ld["rest"], 16)
            for dst, src in ((w_o, wo), (w_g1, wg1), (ln_wb, lnwb), (w_route, gwt), (w_sgu, sgu)):
                sp.dma_start(dst[:, :, :], src).then_inc(ld["rest"], 16)
            load_patches(1)
            sp.dma_start(W[:, 0:LATE * WX], wx[:, 0:LATE * WX]).then_inc(ld["lists"], 16)
            sp.wait_ge(ini, 3)
            for c in range(CH):
                sp.dma_start(sums_d[c].rearrange("(a p) n -> p a n", p=P),
                             padrow[:, 0:D].unsqueeze(1).to_broadcast([P, OUT_ROWS // P, D])).then_inc(ini_d, 16)
            sp.dma_start(rows_d[DUMMY_ROW:DUMMY_ROW + P, :], padrow[:, :]).then_inc(ini_d, 16)
            sp.wait_ge(emb_ps, len(BLOCKS[0]))
            load_patches(2)
            sp.wait_ge(slot_ok, NT)
            sp.dma_start(W[:, LATE * WX:LISTS * WX], wx[:, LATE * WX:LISTS * WX]).then_inc(ld["late"], 16)
            sp.wait_ge(pad_ok, 1)
            with sp.Fori(0, LISTS) as e:
                row = sp.value_load(pad_at[0:1, bass.ds(e, 1)], min_val=0, max_val=DUMMY_ROW - P)
                sp.dma_start(rows_d[bass.ds(row, P), :], padrow[:, :]).then_inc(pads, 16)
            sp.wait_ge(scat, 16 * NT * CHOICES)
            sp.wait_ge(pads, 16 * LISTS)
            sp.wait_ge(ini_d, 16 * (CH + 1))
            sp.wait_ge(table_ok, 1)

            def load_rows(i, u=None):
                u = i if u is None else u
                if not isinstance(i, int) or i >= 4:
                    sp.wait_ge(T_ps, i - 3)
                    sp.wait_ge(meta_ok, i - 3)
                else:
                    sp.wait_ge(en_ok, 4 * NT)
                row = sp.value_load(table[0:1, 1, bass.ds(i, 1)], min_val=0, max_val=DUMMY_ROW)
                sp.dma_start(G[:, u % 4, :], rows_d[bass.ds(row, P), :]).then_inc(g_ld[u % 4], 16)

            groups(sp, load_rows, XT)
            for c in range(CH):
                sp.wait_ge(added[c], 16 * (XT // CH))
            r = 0
            for t, n in enumerate(TILES):
                if t >= 2:
                    sp.wait_ge(fin_ok, t - 1)
                for c in range(CH):
                    sp.dma_start(acc[0:n, t % 2, c, :], sums_d[c][r:r + n, :]).then_inc(fin_ld[t % 2], 16)
                r += n
            r = 0
            for t, n in enumerate(TILES):
                sp.wait_ge(fin_ok, t + 1)
                sp.dma_start(out[r:r + n, :], h[0:n, t, :]).then_inc(out_st, 16)
                r += n
            sp.wait_ge(out_st, 16 * NT)

        @block.gpsimd
        def _(pool):
            pool.memset(ones[:, :], 1.0).then_inc(ini, 1)
            pool.memset(padrow[:, 0:ROW - 1], 0.0)
            pool.iota(padrow_i[:, ROW - 1:ROW], pattern=[[0, 1]], base=TOKENS, channel_multiplier=1).then_inc(ini, 1)
            pool.memset(xrow[:, :, D + EXPERTS:D + LISTS], ANCHOR_ALPHA)
            pool.iota(xrow_i[:, :, ROW - 1], pattern=[[TT, NT]], base=0, channel_multiplier=1).then_inc(ini, 1)
            pool.wait_ge(ini, 3)
            for t, n in enumerate(TILES):
                pool.wait_ge(slot_ok, t + 1)
                for j in range(CHOICES):
                    pool.indirect_dma_start(rows_d, bass.IndirectOffsetOnAxis(ap=slot[0:n, t, j:j + 1], axis=0),
                                            xrow[0:n, t, :], None).then_inc(scat, 16)

            def add_rows(i, u=None):
                c = i % CH if u is None else u
                pool.wait_ge(Y_ok, i + 1)
                if not isinstance(i, int) or i >= CH:
                    pool.wait_ge(added[c], (i - c) * (16 // CH))
                pool.nop(nofuse=True)
                pool.tensor_copy(tok[:, c:c + 1], tok_of[:, bass.ds(i, 1)]).then_inc(tok_ok, 1)
                pool.wait_ge(tok_ok, i + 1)
                pool.nop(nofuse=True)
                pool.indirect_dma_start(sums_d[c], bass.IndirectOffsetOnAxis(ap=tok[:, c:c + 1], axis=0),
                                        Y[:, c, :], None, compute_op=ALU.add).then_inc(added[c], 16)

            groups(pool, add_rows, XT)

        @block.tensor
        def _(pe):
            def out_project(t):
                n = TILES[t]
                pe.wait_ge(ynT_ok, t + 1)
                if t >= 2:
                    pe.wait_ge(h2_ok, t - 1)
                for k in range(KC):
                    m = pe.matmul(B[4 + t % 2][0:n, 0:D], ynT[:, t % 2, k, 0:n], w_o[:, k, :],
                                  start=k == 0, stop=k == KC - 1)
                m.then_inc(wo_ps, 1)

            def route(t):
                n, r = TILES[t], t * TT
                pe.wait_ge(x2T_ok, t + 1)
                if t >= 2:
                    pe.wait_ge(rt_ok, t - 1)
                for k in range(KC):
                    m = pe.matmul(B[t % 2][0:n, 0:EXPERTS], x2T[:, k, r:r + n], w_route[:, k, :],
                                  start=k == 0, stop=k == KC - 1)
                m.then_inc(rt_ps, 1)

            def rank(t):
                n = TILES[t]
                pe.wait_ge(ch_ok, t + 1)
                if t >= 2:
                    pe.wait_ge(slot_ok, t - 1)
                pe.matmul(B[2 + t % 2][0:n, 0:LISTS], before[0:n, 0:n], chosen[0:n, t % 2, :], start=True, stop=True)
                pe.matmul(B[2 + t % 2][:, 64:64 + LISTS], ones[0:n, :], chosen[0:n, t % 2, :],
                          start=True, stop=True).then_inc(rank_ps, 1)

            def embed(t):
                n, b = TILES[t], t // 4
                for c in range(PC):
                    m = pe.matmul(B[t % 2][0:n, 0:D], patches[:, b % 2, c, cols(t):cols(t) + n], w_patch[:, c, :],
                                  start=c == 0, stop=c == PC - 1)
                m.then_inc(emb_ps, 1)

            def transpose2(bank, src, n, done):
                for k in range(KC):
                    m = pe.transpose(bank[:, k * TT:k * TT + n], src[0:n, k * P:(k + 1) * P], ident[0:n, 0:n])
                m.then_inc(done, 1)

            def project(t):
                n = TILES[t]
                for ps, lo, hi, done in ((B[4 + t % 2], 0, 2 * D, qk_ps), (B[6 + t % 2], 2 * D, 3 * D, v_ps)):
                    for k in range(KC):
                        m = pe.matmul(ps[0:n, 0:hi - lo], xnT[:, k, cols(t):cols(t) + n], w_qkv[:, k, lo:hi],
                                      start=k == 0, stop=k == KC - 1)
                    m.then_inc(done, 1)
                if t >= 2:
                    pe.wait_ge(gate_ok, t - 1)
                for k in range(KC):
                    m = pe.matmul(B[t % 2][0:HD, D:D + n], w_g1[:, k, :], xnT[:, k, cols(t):cols(t) + n],
                                  start=k == 0, stop=k == KC - 1)
                m.then_inc(g1_ps, 1)

            def gate(t):
                n = TILES[t]
                pe.wait_ge(g1_ok, t + 1)
                if t >= 2:
                    pe.wait_ge(gate_ok, t - 1)
                pe.matmul(B[t % 2][0:n, 0:D], g1T[:, t % 2, 0:n], w_g2[:, :], start=True, stop=True).then_inc(gate_ps, 1)

            def qk_transpose(t):
                n = TILES[t]
                pe.wait_ge(rope_ok, t + 1)
                if t >= 2:
                    pe.wait_ge(qh_ok, t - 1)
                    pe.wait_ge(kT_ok, t - 1)
                for k in range(2 * KC):
                    m = pe.transpose(B[2 + t % 2][:, k * TT:k * TT + n], qk[0:n, t % 4, k * P:(k + 1) * P],
                                     ident[0:n, 0:n])
                m.then_inc(qkT_ps, 1)

            def energies(t):
                n = TILES[t]
                pe.wait_ge(qh_ok, t + 1)
                pe.wait_ge(kT_ok, t + 1)
                for g in range(4):
                    if t >= 1:
                        pe.wait_ge(en_ok, 4 * t - 3 + g)
                    pe.matmul(B[4 + g][0:n, 0:4 * n], kT[:, t % 2, g // 2, 0:n],
                              q_heads[:, t % 2, 4 * g:4 * g + 4, 0:n],
                              start=True, stop=True).then_inc(en_ps, 1)

            def attend(t):
                n = TILES[t]
                pe.wait_ge(en_ok, 4 * t + 4)
                if t >= 2:
                    pe.wait_ge(og_ok, t - 1)
                for hd in range(HEADS):
                    m = pe.matmul(B[t % 2][0:n, hd * HD:(hd + 1) * HD], energy[0:n, t % 2, hd, 0:n],
                                  v_sb[0:n, t % 4, hd * HD:(hd + 1) * HD], start=True, stop=True)
                m.then_inc(av_ps, 1)

            pe.wait_ge(ld["first"], 16 * 3)
            for b, tiles in enumerate(BLOCKS):
                t0, t1 = tiles[0], tiles[-1] + 1
                pe.wait_ge(ld[f"patch{b}"], 16)
                if b:
                    pe.wait_ge(rt_ok, t0)
                for t in tiles:
                    if t >= 2:
                        pe.wait_ge(h_emb, t - 1)
                    embed(t)
                if b == 0:
                    pe.wait_ge(ld["consts"], 16 * 4)
                    pe.wait_ge(ini, 3)
                else:
                    pe.wait_ge(slot_ok, t0)
                for t in tiles:
                    pe.wait_ge(xn_ok, t + 1)
                    if t >= 2:
                        pe.wait_ge(xnT_ok, t - 1)
                    transpose2(B[2 + t % 2], xn[:, t % 4, :], TILES[t], xnT_ps)
                if b == 0:
                    pe.wait_ge(ld["rest"], 16 * 11)
                else:
                    pe.wait_ge(h2_ok, t0)
                    pe.wait_ge(x2T_ok, t0)
                for t in tiles:
                    pe.wait_ge(xnT_ok, t + 1)
                    if t >= 2:
                        pe.wait_ge(qk_ok, t - 1)
                        pe.wait_ge(v_ok, t - 1)
                        pe.wait_ge(g1_ok, t - 1)
                    project(t)
                    if t > t0:
                        gate(t - 1)
                gate(t1 - 1)
                pe.wait_ge(qk_ok, t1)
                pe.wait_ge(v_ok, t1)
                pe.wait_ge(xnT_ok, t1)
                qk_transpose(t0)
                for t in tiles:
                    if t + 1 < t1:
                        qk_transpose(t + 1)
                    energies(t)
                    if t == t0:
                        pe.wait_ge(gate_ok, t1)
                    if t > t0:
                        attend(t - 1)
                attend(t1 - 1)
                pe.wait_ge(qh_ok, t1)
                for t in tiles:
                    pe.wait_ge(yn_ok, t + 1)
                    if t >= 2:
                        pe.wait_ge(ynT_ok, t - 1)
                    transpose2(B[2 + t % 2], xn[:, t % 4, :], TILES[t], ynT_ps)
                    if t > t0:
                        out_project(t - 1)
                out_project(t1 - 1)
                for t in tiles:
                    pe.wait_ge(x2_ok, t + 1)
                    if t >= 2:
                        pe.wait_ge(x2T_ok, t - 1)
                    transpose2(B[6 + t % 2], xrow[:, t, :], TILES[t], x2T_ps)
                    if t > t0:
                        route(t - 1)
                route(t1 - 1)
                for t in tiles:
                    rank(t)

            def s_up(t):
                n, r = TILES[t], t * TT
                if t >= 2:
                    pe.wait_ge(sh_ok, t - 1)
                for k in range(KC):
                    m = pe.matmul(B[4 + t % 2][0:n, 0:D], x2T[:, k, r:r + n], w_sgu[:, k, :],
                                  start=k == 0, stop=k == KC - 1)
                m.then_inc(sgu_ps, 1)

            def s_transpose(t):
                n = TILES[t]
                pe.wait_ge(sh_ok, t + 1)
                if t >= 2:
                    pe.wait_ge(shT_ok, t - 1)
                pe.transpose(B[6 + t % 2][:, 0:n], H[0:n, t % 2, :], ident[0:n, 0:n]).then_inc(shT_ps, 1)

            def s_down(t):
                n = TILES[t]
                pe.wait_ge(shT_ok, t + 1)
                if t >= 2:
                    pe.wait_ge(hs_ok, t - 1)
                pe.matmul(B[t % 2][0:n, 0:D], HT[:, t % 2, 0:n], w_sd[:, :],
                          start=True, stop=True).then_inc(sd_ps, 1)

            pe.wait_ge(h2_ok, NT)
            pe.wait_ge(x2T_ok, NT)
            pe.wait_ge(rt_ok, NT)
            for t in range(NT):
                s_up(t)
                if t >= 1:
                    s_transpose(t - 1)
                if t >= 2:
                    s_down(t - 2)
            s_transpose(NT - 1)
            s_down(NT - 2)
            s_down(NT - 1)
            pe.wait_ge(cols_ok, 1)
            for q in range(2):
                m = pe.matmul(B[2][0:1, q * P:(q + 1) * P], tcol[:, q:q + 1], ident[:, :], start=True, stop=True)
            m.then_inc(table_ps, 1)

            pe.wait_ge(ld["lists"], 16)
            pe.wait_ge(ld["late"], 16)
            pe.wait_ge(table_ok, 1)
            pe.wait_ge(hs_ok, NT)
            pe.wait_ge(shT_ok, NT)

            def turn_rows(i, u):
                if not isinstance(i, int) or i >= 2:
                    pe.wait_ge(gt_ok, i - 1)
                pe.wait_ge(g_ld[u % 4], (i - u % 4) * 4 + 16)
                for k in range(KC):
                    m = pe.transpose(B[u % 2][:, k * P:(k + 1) * P], G[:, u % 4, k * P:(k + 1) * P], ident[:, :])
                m.then_inc(T_ps, 1)

            def up(i, u, e):
                pe.wait_ge(gt_ok, i + 1)
                for k in range(KC):
                    m = pe.matmul(B[2 + u % 2][:, 0:D], GT[:, u % 2, k, :], W[:, bass.ds(e * WX + k * D, D)],
                                  start=k == 0, stop=k == KC - 1)
                m.then_inc(U_ps, 1)

            def turn_hidden(i, u):
                pe.wait_ge(H_ok, i + 1)
                pe.transpose(B[4 + u % 2][:, 0:P], H[:, u % 2, :], ident[:, :]).then_inc(HT_ps, 1)

            def down(i, u, e):
                pe.wait_ge(HT_ok, i + 1)
                if not isinstance(i, int) or i >= 2:
                    pe.wait_ge(Y_ok, i - 1)
                pe.matmul(B[6 + u % 2][:, 0:D], HT[:, u % 2, :], W[:, bass.ds(e * WX + KC * D, D)],
                          start=True, stop=True).then_inc(D_ps, 1)

            def list_of(i):
                return pe.value_load(table[0:1, 0, bass.ds(i, 1)], min_val=0, max_val=LISTS - 1)

            def list_tile(i, u=None, last=False):
                u = i if u is None else u + 4
                if not isinstance(i, int) or i + 1 < XT:
                    turn_rows(i + 1, u + 1)
                up(i, u, list_of(i))
                if not isinstance(i, int) or i >= 1:
                    turn_hidden(i - 1, u - 1)
                if not isinstance(i, int) or i >= 2:
                    down(i - 2, u - 2, list_of(i - 2))

            turn_rows(0, 0)
            groups(pe, list_tile, XT)
            turn_hidden(XT - 1, XT - 1)
            down(XT - 2, XT - 2, list_of(XT - 2))
            down(XT - 1, XT - 1, list_of(XT - 1))

        @block.scalar
        def _(act):
            def gate_tanh(t):
                n = TILES[t]
                act.wait_ge(gate_ps, t + 1)
                act.activation(gate_th[0:n, t % 4, :], B[t % 2][0:n, 0:D], ACT.Tanh, scale=0.5).then_inc(gate_ok, 1)

            def copy2(dst, bank, n, s, v, done):
                act.wait_ge(s, v)
                act.copy(dst, bank[:, 0:KC * TT].rearrange("p (k t) -> p k t", k=KC)[:, :, 0:n]).then_inc(done, 1)

            for b, tiles in enumerate(BLOCKS):
                t0, t1 = tiles[0], tiles[-1] + 1
                for t in tiles:
                    copy2(xnT[:, :, cols(t):cols(t) + TILES[t]], B[2 + t % 2], TILES[t], xnT_ps, t + 1, xnT_ok)
                for t in tiles:
                    n = TILES[t]
                    act.wait_ge(qk_ps, t + 1)
                    act.activation(qk[0:n, t % 4, :], B[4 + t % 2][0:n, :], ACT.Silu).then_inc(qk_ok, 1)
                    act.wait_ge(v_ps, t + 1)
                    act.copy(v_sb[0:n, t % 4, :], B[6 + t % 2][0:n, 0:D]).then_inc(v_ok, 1)
                    act.wait_ge(g1_ps, t + 1)
                    if t >= 2:
                        act.wait_ge(gate_ps, t - 1)
                    act.copy(g1T[:, t % 2, 0:n], B[t % 2][0:HD, D:D + n]).then_inc(g1_ok, 1)
                    if t > t0:
                        gate_tanh(t - 1)
                gate_tanh(t1 - 1)
                for t in tiles:
                    n = TILES[t]
                    act.wait_ge(qkT_ps, t + 1)
                    if t >= 2:
                        act.wait_ge(en_ps, 4 * (t - 1))
                    act.copy(kT[:, t % 2, :, 0:n], B[2 + t % 2][:, KC * TT:2 * KC * TT]
                             .rearrange("p (k t) -> p k t", k=KC)[:, :, 0:n]).then_inc(kT_ok, 1)
                for t in tiles:
                    n = TILES[t]
                    act.wait_ge(ynT_ps, t + 1)
                    if t >= 2:
                        act.wait_ge(wo_ps, t - 1)
                    for k in range(KC):
                        m = act.activation(ynT[:, t % 2, k, 0:n], B[2 + t % 2][:, k * TT:k * TT + n], ACT.Identity,
                                           scale=ln_wb[:, k, 0:1], bias=ln_wb[:, k, 1:2])
                    m.then_inc(ynT_ok, 1)
                for t in tiles:
                    n, r = TILES[t], t * TT
                    copy2(x2T[:, :, r:r + n], B[6 + t % 2], n, x2T_ps, t + 1, x2T_ok)
                for t in tiles:
                    n = TILES[t]
                    act.wait_ge(rt_ps, t + 1)
                    if t >= 2:
                        act.wait_ge(slot_ok, t - 1)
                    act.activation(sig[0:n, t % 2, :], B[t % 2][0:n, 0:EXPERTS], ACT.Sigmoid).then_inc(rt_ok, 1)
            def s_silu(t):
                n = TILES[t]
                act.wait_ge(sgu_ps, t + 1)
                if t >= 2:
                    act.wait_ge(sh_ok, t - 1)
                act.activation(S[0:n, t % 2, :], B[4 + t % 2][0:n, 0:P], ACT.Silu).then_inc(ssilu_ok, 1)

            def s_copy(t):
                n = TILES[t]
                act.wait_ge(shT_ps, t + 1)
                if t >= 2:
                    act.wait_ge(sd_ps, t - 1)
                act.copy(HT[:, t % 2, 0:n], B[6 + t % 2][:, 0:n]).then_inc(shT_ok, 1)

            act.wait_ge(rope_ok, NT)
            for t in range(NT):
                s_silu(t)
                if t >= 1:
                    s_copy(t - 1)
            s_copy(NT - 1)

            def hidden_silu(i, u=None):
                v = i if u is None else u
                act.wait_ge(U_ps, i + 1)
                if not isinstance(i, int) or i >= 2:
                    act.wait_ge(H_ok, i - 1)
                act.activation(S[:, v % 2, :], B[2 + v % 2][:, 0:P], ACT.Silu).then_inc(silu_ok, 1)
                if not isinstance(i, int) or i >= 2:
                    weigh(i - 2, v + 2)

            def weigh(i, v):
                act.wait_ge(D_ps, i + 1)
                act.wait_ge(meta_ok, i + 1)
                if not isinstance(i, int) or i >= CH:
                    act.wait_ge(added[v % 4], (i - v % 4) * (16 // CH))
                act.activation(Y[:, v % 4, :], B[6 + v % 2][:, 0:D], ACT.Copy, scale=wcol[:, bass.ds(i, 1)]).then_inc(Y_ok, 1)

            groups(act, hidden_silu, XT)
            weigh(XT - 2, XT - 2)
            weigh(XT - 1, XT - 1)

        @block.vector
        def _(dve):
            count = [0]

            def step(ins):
                count[0] += 1
                ins.then_inc(dchain, 1)
                dve.wait_ge(dchain, count[0])

            def stat(src, t):
                n = TILES[t]
                step(dve.bn_stats(stats[0:n, t % 4, :], src))
                step(dve.bn_aggr(mv[0:n, t % 4, :], stats[0:n, t % 4, :]))

            def rsqrt(k, eps):
                v, y, a = nwt[:, 0, 0:k], nwt[:, 1, 0:k], nwt[:, 2, 0:k]
                vi, yi, ai_ = nwt_i[:, 0, 0:k], nwt_i[:, 1, 0:k], nwt_i[:, 2, 0:k]
                step(dve.tensor_scalar(v, mv[:, 0:k, 1], eps, None, ALU.add))
                step(dve.tensor_scalar(ai_, vi, 1, None, ALU.logical_shift_right))
                step(dve.tensor_scalar(yi, ai_, -1.0, float(0x5F3759DF), ALU.mult, ALU.add))
                for _ in range(3):
                    step(dve.scalar_tensor_tensor(a, y, -0.5, y, ALU.mult, ALU.mult))
                    step(dve.tensor_tensor(a, a, v, ALU.mult))
                    step(dve.scalar_tensor_tensor(y, a, 1.5, y, ALU.add, ALU.mult))

            def normal(dst, src, t, done):
                n = TILES[t]
                dve.tensor_scalar(dst, src, mv[0:n, t % 4, 0:1], nwt[0:n, 1, t % 4:t % 4 + 1],
                                  ALU.subtract, ALU.mult).then_inc(done, 1)

            def choose(t):
                n, u = TILES[t], t % 2
                s = sig[0:n, u, :]
                sct, g0, g1, g2, g3 = sc[0:n, :], gs[0:n, 0, :], gs[0:n, 1, :], gs[0:n, 2, :], gs[0:n, 3, :]
                by_group = sct.rearrange("p (g e) -> p g e", g=GROUPS)

                def inner(v, k):
                    return v.unsqueeze(2).to_broadcast([n, v.shape[1], k])

                def outer(v, k):
                    return v.unsqueeze(1).to_broadcast([n, k, v.shape[1]])

                dve.wait_ge(rt_ok, t + 1)
                if t >= 2:
                    dve.wait_ge(rank_ps, t - 1)
                step(dve.tensor_tensor(sct, s, bias_rt[0:n, :], ALU.add))
                for g in range(GROUPS):
                    m = dve.max(top8[0:n, g, :], by_group[:, g, :])
                step(m)
                step(dve.tensor_tensor(g0, top8[0:n, :, 0], top8[0:n, :, 1], ALU.add))
                dve.tensor_tensor(cmp[0:n, 0], outer(g0, GROUPS), inner(g0, GROUPS), ALU.is_gt)
                step(dve.tensor_tensor(cmp[0:n, 1], outer(g0, GROUPS), inner(g0, GROUPS), ALU.is_equal))
                step(dve.tensor_tensor(cmp[0:n, 1], cmp[0:n, 1], tri4[0:n, :].rearrange("p (a b) -> p a b", a=GROUPS),
                                       ALU.mult))
                step(dve.tensor_tensor(cmp[0:n, 0], cmp[0:n, 0], cmp[0:n, 1], ALU.add))
                step(dve.reduce_sum(g1, cmp[0:n, 0], axis=AX.X))
                step(dve.tensor_scalar(g2, g1, 2.0, None, ALU.is_lt))
                step(dve.tensor_scalar(g3, g2, BIG, -BIG, ALU.mult, ALU.add))
                step(dve.tensor_tensor(by_group, by_group, inner(g2, GE), ALU.mult))
                step(dve.tensor_tensor(by_group, by_group, inner(g3, GE), ALU.add))
                step(dve.max(tv[0:n, :], sct))
                step(dve.max_index(ti[0:n, :], tv[0:n, :], sct))
                dve.tensor_copy(idx[0:n, 0:TOPK], ti[0:n, 0:TOPK])
                step(dve.tensor_scalar(ai[0:n, :], ti[0:n, 0:1], 1, None, ALU.logical_shift_right))
                step(dve.tensor_scalar(idx[0:n, TOPK:CHOICES], ai[0:n, :], float(EXPERTS), None, ALU.add))
                step(dve.tensor_tensor(oh[0:n, u], inner(idx[0:n, :], LISTS), outer(iota_l[0:n, :], CHOICES), ALU.is_equal))
                dve.reduce_sum(chosen[0:n, u, :], oh[0:n, u].rearrange("p j e -> p e j"), axis=AX.X).then_inc(ch_ok, 1)
                dve.wait_ge(ch_ok, t + 1)
                w = xrow[0:n, t, D:D + EXPERTS]
                step(dve.tensor_tensor(w, chosen[0:n, u, 0:EXPERTS], s, ALU.mult))
                step(dve.reduce_sum(wsum[0:n, 0:1], w, axis=AX.X))
                step(dve.tensor_scalar(wsum[0:n, 0:1], wsum[0:n, 0:1], 1e-20, None, ALU.add))
                step(dve.reciprocal(wsum[0:n, 1:2], wsum[0:n, 0:1]))
                step(dve.tensor_scalar(w, w, wsum[0:n, 1:2], ROUTED_SCALE, ALU.mult, ALU.mult))

            def place(t):
                n, u = TILES[t], t % 2
                dve.wait_ge(rank_ps, t + 1)
                step(dve.tensor_tensor(rnk[0:n, :], B[2 + u][0:n, 0:LISTS], base[0:n, :], ALU.add))
                dve.tensor_tensor(base[:, :], base[:, :], B[2 + u][:, 64:64 + LISTS], ALU.add)
                step(dve.tensor_tensor(prod[0:n], oh[0:n, u], rnk[0:n, :].unsqueeze(1).to_broadcast([n, CHOICES, LISTS]),
                                       ALU.mult))
                step(dve.reduce_sum(slot_f[0:n, :], prod[0:n], axis=AX.X))
                dve.tensor_copy(slot[0:n, t, :], slot_f[0:n, :]).then_inc(slot_ok, 1)
                dve.wait_ge(slot_ok, t + 1)

            step(dve.memset(mv[:, :, :], 1.0))
            dve.wait_ge(ld["first"], 16 * 3)
            step(dve.tensor_tensor(posb[:, :], posb[:, :], brow_sb[:, :], ALU.add))
            for b, tiles in enumerate(BLOCKS):
                t0, t1 = tiles[0], tiles[-1] + 1
                for t in tiles:
                    n = TILES[t]
                    dve.wait_ge(emb_ps, t + 1)
                    dve.tensor_tensor(h[0:n, t, :], B[t % 2][0:n, 0:D], posb[0:n, :], ALU.add).then_inc(h_emb, 1)
                    dve.wait_ge(h_emb, t + 1)
                    stat(h[0:n, t, :], t)
                rsqrt(len(tiles), EPS)
                if b:
                    dve.wait_ge(ynT_ps, t0)
                for t in tiles:
                    normal(xn[0:TILES[t], t % 4, :], h[0:TILES[t], t, :], t, xn_ok)
                if b == 0:
                    dve.wait_ge(ld["consts"], 16 * 4)
                for t in tiles:
                    n = TILES[t]
                    dve.wait_ge(qk_ok, t + 1)
                    q = qk[0:n, t % 4, :].rearrange("p (h d) -> p h d", d=HD)
                    a = rp[0:n, 0, :].rearrange("p (h d) -> p h d", d=HD)
                    r_ = rp[0:n, 1, :].rearrange("p (h d) -> p h d", d=HD)
                    half = HD // 2

                    def tab(i, lo, hi):
                        return cossin[0:n, i, lo:hi].unsqueeze(1).to_broadcast([n, 2 * HEADS, hi - lo])

                    dve.tensor_tensor(a, q, tab(0, 0, HD), ALU.mult)
                    dve.tensor_tensor(r_[:, :, 0:half], q[:, :, half:HD], tab(1, 0, half), ALU.mult)
                    step(dve.tensor_tensor(r_[:, :, half:HD], q[:, :, 0:half], tab(1, half, HD), ALU.mult))
                    dve.tensor_tensor(q, a, r_, ALU.add).then_inc(rope_ok, 1)
                    dve.wait_ge(rope_ok, t + 1)
                if b == 0:
                    dve.wait_ge(ld["rest"], 16 * 11)

                def split_heads(t):
                    n = TILES[t]
                    dve.wait_ge(kT_ok, t + 1)
                    if t >= 2:
                        dve.wait_ge(en_ps, 4 * (t - 1))
                    for k in range(KC):
                        m = dve.tensor_tensor(
                            q_heads[:, t % 2, 8 * k:8 * k + 8, 0:n],
                            B[2 + t % 2][:, k * TT:k * TT + n].unsqueeze(1).to_broadcast([P, 8, n]),
                            hmask[:, :].unsqueeze(2).to_broadcast([P, 8, n]), ALU.mult)
                    m.then_inc(qh_ok, 1)

                def mask_energy(t):
                    n = TILES[t]
                    if t >= 2:
                        dve.wait_ge(av_ps, t - 1)
                    for g in range(4):
                        dve.wait_ge(en_ps, 4 * t + g + 1)
                        dve.tensor_tensor(energy[0:n, t % 2, 4 * g:4 * g + 4, 0:n],
                                          B[4 + g][0:n, 0:4 * n].rearrange("p (h t) -> p h t", h=4),
                                          causal[0:n, 0:n].unsqueeze(1).to_broadcast([n, 4, n]),
                                          ALU.mult).then_inc(en_ok, 1)

                def apply_gate(t):
                    n = TILES[t]
                    dve.wait_ge(av_ps, t + 1)
                    dve.wait_ge(gate_ok, t + 1)
                    dve.scalar_tensor_tensor(xn[0:n, t % 4, :], gate_th[0:n, t % 4, :], 1.0,
                                             B[t % 2][0:n, 0:D], ALU.add, ALU.mult).then_inc(og_ok, 1)
                    dve.wait_ge(og_ok, t + 1)
                    stat(xn[0:n, t % 4, :], t)

                split_heads(t0)
                for t in tiles:
                    if t + 1 < t1:
                        split_heads(t + 1)
                    mask_energy(t)
                    if t > t0:
                        apply_gate(t - 1)
                apply_gate(t1 - 1)
                rsqrt(len(tiles), 4 * EPS)
                for t in tiles:
                    normal(xn[0:TILES[t], t % 4, :], xn[0:TILES[t], t % 4, :], t, yn_ok)
                for t in tiles:
                    n = TILES[t]
                    dve.wait_ge(wo_ps, t + 1)
                    dve.tensor_tensor(h[0:n, t, :], B[4 + t % 2][0:n, 0:D], h[0:n, t, :], ALU.add).then_inc(h2_ok, 1)
                    dve.wait_ge(h2_ok, t + 1)
                    stat(h[0:n, t, :], t)
                rsqrt(len(tiles), EPS)
                if b == 0:
                    dve.wait_ge(ini, 3)
                for t in tiles:
                    normal(xrow[0:TILES[t], t, 0:D], h[0:TILES[t], t, :], t, x2_ok)
                if b == 0:
                    step(dve.tensor_copy(base[:, :], base0))
                for t in tiles:
                    choose(t)
                    if t > t0:
                        place(t - 1)
                place(t1 - 1)
            counts, tiles_of, ends, starts, t4, t5 = (tabf[:, q, :] for q in range(6))
            step(dve.tensor_tensor(counts, base[:, :], base0, ALU.subtract))
            dve.tensor_copy(pad_at[:, :], base[0:1, :]).then_inc(pad_ok, 1)
            step(dve.tensor_scalar(cnt_i[:, :], counts, float(P - 1), None, ALU.add))
            step(dve.tensor_scalar(cnt_i[:, :], cnt_i[:, :], 7, None, ALU.logical_shift_right))
            step(dve.tensor_copy(tiles_of, cnt_i[:, :]))
            dve.tensor_tensor_scan(ends[:, 0:EXPERTS], ones[:, 0:EXPERTS], tiles_of[:, 0:EXPERTS], 0.0, ALU.mult, ALU.add)
            step(dve.tensor_tensor_scan(ends[:, EXPERTS:LISTS], ones[:, 0:ANCHORS], tiles_of[:, EXPERTS:LISTS],
                                        float(ROUTED_TILES), ALU.mult, ALU.add))
            step(dve.tensor_tensor(starts, ends, tiles_of, ALU.subtract))
            dve.tensor_scalar(t4, starts, pcol, None, ALU.is_le)
            step(dve.tensor_scalar(t5, ends, pcol, None, ALU.is_gt))
            step(dve.tensor_tensor(t4, t4, t5, ALU.mult))
            dve.reduce_sum(tcol[:, 2:3], t4, axis=AX.X)
            step(dve.tensor_tensor(t5, t4, iota_l, ALU.mult))
            dve.reduce_sum(tcol[:, 0:1], t5, axis=AX.X)
            step(dve.scalar_tensor_tensor(starts, starts, -float(P), base0, ALU.mult, ALU.add))
            step(dve.tensor_tensor(t4, t4, starts, ALU.mult))
            step(dve.reduce_sum(tcol[:, 1:2], t4, axis=AX.X))
            step(dve.tensor_scalar(tcol[:, 3:4], pcol, float(P), -float(DUMMY_ROW), ALU.mult, ALU.add))
            step(dve.tensor_tensor(tcol[:, 3:4], tcol[:, 3:4], tcol[:, 2:3], ALU.mult))
            dve.scalar_tensor_tensor(tcol[:, 1:2], tcol[:, 3:4], float(DUMMY_ROW), tcol[:, 1:2],
                                     ALU.add, ALU.add).then_inc(cols_ok, 1)

            def s_mult(t):
                n = TILES[t]
                dve.wait_ge(ssilu_ok, t + 1)
                if t >= 2:
                    dve.wait_ge(shT_ps, t - 1)
                dve.tensor_tensor(H[0:n, t % 2, :], S[0:n, t % 2, :], B[4 + t % 2][0:n, P:2 * P],
                                  ALU.mult).then_inc(sh_ok, 1)

            def s_add(t):
                n = TILES[t]
                dve.wait_ge(sd_ps, t + 1)
                dve.tensor_tensor(h[0:n, t, :], B[t % 2][0:n, 0:D], h[0:n, t, :], ALU.add).then_inc(hs_ok, 1)

            dve.wait_ge(ynT_ps, NT)
            for t in range(NT):
                s_mult(t)
                if t >= 2:
                    s_add(t - 2)
            s_add(NT - 2)
            s_add(NT - 1)
            dve.wait_ge(table_ps, 1)
            dve.tensor_copy(table[:, :, :].rearrange("p a b -> p (a b)"), B[2][0:1, 0:2 * P]).then_inc(table_ok, 1)
            dve.wait_ge(table_ok, 1)

            def tile_steps(i, u=None):
                v = i if u is None else u
                dyn = not isinstance(i, int)
                dve.wait_ge(T_ps, i + 1)
                if dyn or i >= 2:
                    dve.wait_ge(U_ps, i - 1)
                dve.tensor_copy(GT[:, v % 2, :, :].rearrange("p k s -> p (k s)"), B[v % 2][:, 0:D]).then_inc(gt_ok, 1)
                e = dve.value_load(table[0:1, 0, bass.ds(i, 1)], min_val=0, max_val=LISTS - 1)
                dve.tensor_copy(wcol[:, bass.ds(i, 1)], G[:, v % 4, bass.ds(D + e, 1)])
                dve.tensor_copy(tok_of[:, bass.ds(i, 1)], G_i[:, v % 4, ROW - 1:ROW]).then_inc(meta_ok, 1)
                if dyn or i >= 1:
                    turn(i - 1, v + 3)

            def turn(i, v):
                dve.wait_ge(silu_ok, i + 1)
                if not isinstance(i, int) or i >= 2:
                    dve.wait_ge(HT_ps, i - 1)
                dve.tensor_tensor(H[:, v % 2, :], S[:, v % 2, :], B[2 + v % 2][:, P:2 * P], ALU.mult).then_inc(H_ok, 1)
                if not isinstance(i, int) or i >= 1:
                    hidden_copy(i - 1, v + 1)

            def hidden_copy(i, v):
                dve.wait_ge(HT_ps, i + 1)
                if not isinstance(i, int) or i >= 2:
                    dve.wait_ge(D_ps, i - 1)
                dve.tensor_copy(HT[:, v % 2, :], B[4 + v % 2][:, 0:P]).then_inc(HT_ok, 1)

            groups(dve, tile_steps, XT)
            turn(XT - 1, XT - 1)
            hidden_copy(XT - 1, XT - 1)
            for t, n in enumerate(TILES):
                dve.wait_ge(fin_ld[t % 2], 16 * CH * (t // 2 + 1))
                for c in range(CH):
                    m = dve.tensor_tensor(h[0:n, t, :], h[0:n, t, :], acc[0:n, t % 2, c, :], ALU.add)
                    if c < CH - 1:
                        step(m)
                m.then_inc(fin_ok, 1)


def host_layout(a):
    f = {k: np.asarray(v) for k, v in a.items()}

    def chunks(m):
        return m.reshape(-1, P, m.shape[-1]).transpose(1, 0, 2)

    x = f["x"].reshape(IMAGES, 3, 6, 16, 6, 16).transpose(1, 3, 5, 0, 2, 4).reshape(PC * P, IMAGES, PATCHES)
    patches = np.zeros((PC * P, IMAGES, SEQ), x.dtype)
    patches[:, :, 1:] = x
    pos = np.concatenate([f["cls_tok"][0], f["L0_tok_pos_embd"][0]], 0)
    bias = np.zeros((SEQ, D), pos.dtype)
    bias[1:] = f["L0_tok_b"]
    wq, wk, wv = f["L0_attn_Wq"], f["L0_attn_Wk"], f["L0_attn_Wv"]

    def lists(gate, up, down, hidden):
        n = gate.shape[0]
        w = np.zeros((P, n, 3, 2, P), gate.dtype)
        w[:, :, 0:KC, 0, 0:hidden] = gate.reshape(n, KC, P, hidden).transpose(2, 0, 1, 3)
        w[:, :, 0:KC, 1, 0:hidden] = up.reshape(n, KC, P, hidden).transpose(2, 0, 1, 3)
        w[0:hidden, :, KC] = down.transpose(1, 0, 2).reshape(hidden, n, 2, P)
        return w.reshape(P, n * WX)

    wx = np.concatenate([lists(f["L0_ffn_w_gate"], f["L0_ffn_w_up"], f["L0_ffn_w_down"], P),
                         lists(f["L0_ffn_anchor_w_gate"], f["L0_ffn_anchor_w_up"], f["L0_ffn_anchor_w_down"], 64)], 1)
    return dict(
        pt=chunks(patches.reshape(PC * P, TOKENS)), wt=chunks(f["L0_tok_W"].T),
        posr=np.tile(pos, (3, 1)), brow=np.tile(bias, (3, 1)),
        wqkv=chunks(np.concatenate([wq, wk, wv], 1)), wo=chunks(f["L0_attn_Wo"]), wg1=chunks(f["L0_attn_Wg1"]),
        wg2=f["L0_attn_Wg2"], lnwb=chunks(np.stack([f["L0_attn_ln_w"], f["L0_attn_ln_b"]], 1)),
        gwt=chunks(f["L0_ffn_gate_weight"].T), gbias=np.tile(f["L0_ffn_gate_bias"], (P, 1)),
        sgu=chunks(np.concatenate([f["L0_ffn_shared_w_gate"], f["L0_ffn_shared_w_up"]], 1)),
        sd=f["L0_ffn_shared_w_down"], wx=wx)


def constants():
    tok = np.arange(TT)
    img, pos = tok // SEQ, tok % SEQ
    causal = ((img[:, None] == img[None]) & (pos[None] >= pos[:, None])).astype(np.float32)
    hmask = (np.arange(P)[:, None] // HD == np.arange(HEADS // KC)[None]).astype(np.float32)
    inv = (1.0 / np.float32(10000.0) ** (np.arange(0, HD, 2, dtype=np.float32) / np.float32(HD))).astype(np.float32)
    ang = pos.astype(np.float32)[:, None] * inv[None]
    cos, sin = np.cos(ang), np.sin(ang)
    cs = np.stack([np.concatenate([cos, cos], 1), np.concatenate([-sin, sin], 1)], 1)
    before = np.triu(np.ones((P, P), np.float32), 1)
    small = np.zeros((P, 2 * LISTS + 16 + 2), np.float32)
    small[:, 0:LISTS] = np.arange(LISTS)
    small[:, LISTS:2 * LISTS] = np.arange(LISTS) * LIST_ROWS
    small[:, 2 * LISTS:2 * LISTS + 16] = np.tril(np.ones((GROUPS, GROUPS)), -1).ravel()
    small[:, 2 * LISTS + 16] = np.arange(P)
    return dict(ident_c=np.eye(P, dtype=np.float32), cmask_c=causal, hmask_c=hmask, cs_c=cs.astype(np.float32),
                before_c=before, small_c=small)


def kernel(**inputs):
    import concourse.bacc as bacc
    from concourse.bass_utils import run_bass_kernel_spmd

    nc = bacc.Bacc("TRN2", target_bir_lowering=False, num_devices=1)
    arrays, args = {}, {}
    for name, a in {**host_layout(inputs), **constants()}.items():
        a = np.ascontiguousarray(a)
        arrays[f"in_{name}"] = a
        args[name] = nc.dram_tensor(f"in_{name}", a.shape, mybir.dt.from_np(a.dtype), kind="ExternalInput").ap()
    out = nc.dram_tensor("out_h", (TOKENS, D), F32, kind="ExternalOutput").ap()
    build(nc, **args, out=out)
    r = run_bass_kernel_spmd(nc, [arrays], core_ids=[0])
    return r.results[0]["out_h"].reshape(IMAGES, SEQ, D)
```

```python
from contextlib import ExitStack

import numpy as np

import concourse.bass as bass
from concourse import mybir

F32 = mybir.dt.float32
I32 = mybir.dt.int32
U32 = mybir.dt.uint32
ALU = mybir.AluOpType
ACT = mybir.ActivationFunctionType
AX = mybir.AxisListType

P = 128
D = 256
KC = D // P
IMAGES, PATCHES = 32, 36
SEQ = PATCHES + 1
TOKENS = IMAGES * SEQ
PC = 3 * 16 * 16 // P
HEADS, HD = 16, 16
TT = 3 * SEQ
TP = 112
TILES = [TT] * (IMAGES // 3) + [IMAGES % 3 * SEQ]
NT = len(TILES)
BLOCKS = [[0, 1, 2, 3], [4, 5, 6, 7], [8, 9, 10]]
BT = 4 * TT
EPS = 1e-5
EXPERTS, GROUPS, TOPK = 32, 4, 6
GE = EXPERTS // GROUPS
ANCHORS = 16
LISTS = EXPERTS + ANCHORS
CHOICES = TOPK + 1
ROUTED_SCALE, ANCHOR_ALPHA = 0.2, 0.1
WX = 3 * D
LIST_ROWS = TOKENS
DUMMY_ROW = LISTS * LIST_ROWS
ROW = D + LISTS + 1
ROUTED_TILES = (TOKENS * TOPK + EXPERTS * (P - 1)) // P
ANCHOR_TILES = (TOKENS + ANCHORS * (P - 1)) // P
XT = ROUTED_TILES + ANCHOR_TILES
CH = 4
FILL_ROW = NT * TP
SUM_ROWS = 11 * P
LATE = [17, 26, 42, LISTS]
FIN_DVE = 7
assert FILL_ROW + P <= SUM_ROWS
BIG = 3.0e38
assert XT % CH == 0


def cols(t):
    return (t % 4) * TT


def build(nc, pt, wt, posr, brow, wqkv, wo, wg1, wg2, lnwb, gwt, gbias, sgu, sd, wx,
          ident_c, cmask_c, hmask_c, cs_c, before_c, small_c, out):
    with ExitStack() as ctx:
        def sb(name, shape, dt=F32):
            return ctx.enter_context(nc.sbuf_tensor(name, shape, dt))

        def sem(name):
            return ctx.enter_context(nc.semaphore(name))

        W = sb("W", [P, LISTS * WX])
        taken = [LATE[0] * WX]

        def early(shape):
            n = int(np.prod(shape))
            v = W[:, taken[0]:taken[0] + n]
            taken[0] += n
            assert taken[0] <= LISTS * WX
            if len(shape) == 2:
                return v.rearrange("p (a b) -> p a b", b=shape[1])
            if len(shape) == 3:
                return v.rearrange("p (a b c) -> p a b c", b=shape[1], c=shape[2])
            return v

        patches = early([2, PC, BT])
        w_patch = early([PC, D])
        posb = early([D])[0:TT]
        brow_sb = early([D])[0:TT]
        assert taken[0] >= LATE[1] * WX
        w_qkv = early([KC, 3 * D])
        w_g2 = early([D])[0:HD]
        xnT = early([KC, BT])
        qk = early([4, 2 * D])
        rp = early([2, 2 * D])
        v_sb = early([4, D])
        qT = early([2, KC, TT])
        kT = early([2, KC, TT])
        q_heads = early([2, HEADS, TT])
        gate_th = early([4, D])
        assert taken[0] >= LATE[2] * WX
        xn = early([4, D])
        w_o = early([KC, D])
        ynT = early([2, KC, TT])
        oh = early([4, CHOICES, LISTS])
        prod = early([CHOICES, LISTS])

        w_g1 = sb("w_g1", [P, KC, HD])
        ln_wb = sb("ln_wb", [P, KC, 2])
        w_route = sb("w_route", [P, KC, EXPERTS])
        bias_rt = sb("bias_rt", [P, EXPERTS])
        w_sgu = sb("w_sgu", [P, KC, D])
        w_sd = sb("w_sd", [P, D])
        ident = sb("ident", [P, P])
        causal = sb("causal", [TT, TT])
        hmask = sb("hmask", [P, HEADS // KC])
        cossin = sb("cossin", [TT, 2, HD])
        before = sb("before", [P, P])
        ones = sb("ones", [P, P])
        small = sb("small", [P, 2 * LISTS + 16 + 2])
        iota_l, base0, tri4, pcol = (small[:, 0:LISTS], small[:, LISTS:2 * LISTS],
                                     small[:, 2 * LISTS:2 * LISTS + 16], small[:, 2 * LISTS + 16:2 * LISTS + 17])
        h = sb("h", [P, NT, D])
        xrow = sb("xrow", [P, NT, ROW])
        xrow_i = xrow[:, :, :].bitcast(I32)
        x2T = sb("x2T", [P, KC, TOKENS])
        g1T = sb("g1T", [HD, 2, TT])
        e_sb = sb("e_sb", [P, 2 * HEADS * TT])
        energy = e_sb[:, :].rearrange("p (u h t) -> p u h t", u=2, h=HEADS)
        stats = sb("stats", [P, 4, 6])
        mv = sb("mv", [P, 4, 2])
        nwt = sb("nwt", [P, 4, 4])
        nwt_i = nwt[:, :, :].bitcast(I32)
        sig = sb("sig", [P, 4, EXPERTS])
        sc = sb("sc", [P, 4, EXPERTS])
        top8 = sb("top8", [P, 4 * GROUPS, 8])
        gs = sb("gs", [P, 4, 4 * GROUPS])
        cmp = sb("cmp", [P, 2, 4, GROUPS, GROUPS])
        tv = sb("tv", [P, 4, 8])
        ti = sb("ti", [P, 4, 8], U32)
        ai = sb("ai", [P, 4], U32)
        idx = sb("idx", [P, 4, CHOICES])
        chosen = sb("chosen", [P, 4, LISTS])
        base = sb("base", [P, LISTS])
        rnk = sb("rnk", [P, LISTS])
        slot_f = sb("slot_f", [P, CHOICES])
        slot = sb("slot", [P, NT, CHOICES], I32)
        wsum = sb("wsum", [P, 2, 4])
        cnt_i = sb("cnt_i", [P, LISTS], I32)
        tabf = sb("tabf", [P, 6, LISTS])
        tcol = sb("tcol", [P, 8])
        table = sb("table", [1, 3, P], I32)
        fresh, dups = (v[:, :, :].rearrange("p k e -> p (k e)") for v in (sig, sc))
        padrow = sb("padrow", [P, ROW])
        padrow_i = padrow[:, :].bitcast(I32)
        at = [0]

        def later(n):
            v = e_sb[:, at[0]:at[0] + n]
            at[0] += n
            assert at[0] <= 2 * HEADS * TT
            return v

        G = later(4 * ROW).rearrange("p (u r) -> p u r", u=4)
        GT = later(2 * D).rearrange("p (u k s) -> p u k s", u=2, k=KC)
        S = later(2 * P).rearrange("p (u s) -> p u s", u=2)
        H = later(2 * P).rearrange("p (u s) -> p u s", u=2)
        HT = later(2 * P).rearrange("p (u s) -> p u s", u=2)
        Y = later(4 * D).rearrange("p (u s) -> p u s", u=4)
        G_i = G.bitcast(I32)
        wcol = sb("wcol", [P, XT])
        tok_of = sb("tok_of", [P, XT], I32)
        tok = sb("tok", [P, CH], I32)
        sums = W[0:TP, 0:CH * NT * D].rearrange("p (c t d) -> p c t d", c=CH, t=NT)

        B = [ctx.enter_context(nc.psum_tensor(f"B{i}", [P, 512], F32)) for i in range(8)]

        rows_d = nc.dram_tensor("rows_d", [DUMMY_ROW + P, ROW], F32).ap()
        sums_d = [nc.dram_tensor(f"sums{c}_d", [SUM_ROWS, D], F32).ap() for c in range(CH)]

        ld = {n: sem(f"ld_{n}") for n in ("patch1", "patch2", "first", "consts", "rest", "lists", "late0", "late1", "late2")}
        chunk = [sem(f"chunk{c}") for c in range(PC)]
        h_emb, xn_ok, xnT_ok = sem("h_emb"), sem("xn_ok"), sem("xnT_ok")
        emb_ps, xnT_ps, qk_ps, v_ps = sem("emb_ps"), sem("xnT_ps"), sem("qk_ps"), sem("v_ps")
        qk_ok, v_ok, g1_ps, g1_ok = sem("qk_ok"), sem("v_ok"), sem("g1_ps"), sem("g1_ok")
        gate_ps, gate_ok, rope_ok = sem("gate_ps"), sem("gate_ok"), sem("rope_ok")
        qkT_ps, qh_ok, kT_ok, qkT_ok = sem("qkT_ps"), sem("qh_ok"), sem("kT_ok"), sem("qkT_ok")
        en_ps, en_ok, av_ps, og_ok = sem("en_ps"), sem("en_ok"), sem("av_ps"), sem("og_ok")
        yn_ok, ynT_ps, ynT_ok, wo_ps, h2_ok = sem("yn_ok"), sem("ynT_ps"), sem("ynT_ok"), sem("wo_ps"), sem("h2_ok")
        x2_ok, x2T_ps, x2T_ok = sem("x2_ok"), sem("x2T_ps"), sem("x2T_ok")
        rt_ps, rt_ok, ch_ok, ch_done, rank_ps, slot_ok = (sem("rt_ps"), sem("rt_ok"), sem("ch_ok"), sem("ch_done"), sem("rank_ps"), sem("slot_ok"))
        dchain, ln_ok = sem("dchain"), sem("ln_ok")
        ini, ini_d = sem("ini"), sem("ini_d")
        scat, empty = sem("scat"), sem("empty")
        cols_ok, table_ps, table_ok = sem("cols_ok"), sem("table_ps"), sem("table_ok")
        sgu_ps, ssilu_ok, sh_ok, shT_ps, shT_ok, sd_ps, hs_ok = (
            sem("sgu_ps"), sem("ssilu_ok"), sem("sh_ok"), sem("shT_ps"), sem("shT_ok"), sem("sd_ps"), sem("hs_ok"))
        g_ld = [sem(f"g_ld{u}") for u in range(4)]
        T_ps, gt_ok, U_ps, silu_ok, H_ok, HT_ps, HT_ok, D_ps, Y_ok = (
            sem("T_ps"), sem("gt_ok"), sem("U_ps"), sem("silu_ok"), sem("H_ok"), sem("HT_ps"), sem("HT_ok"),
            sem("D_ps"), sem("Y_ok"))
        added = [sem(f"added{c}") for c in range(CH)]
        meta_ok, tok_ok = sem("meta_ok"), sem("tok_ok")
        fin_ld = [sem(f"fin_ld{c}") for c in range(CH)]
        fin_ok, fin_pool, out_st = sem("fin_ok"), sem("fin_pool"), sem("out_st")
        block = ctx.enter_context(nc.Block())

        def group_wait(eng, s, n):
            if n > 0:
                eng.wait_ge(s, n)

        def groups(eng, body, n, lag=0):
            for i in range(4):
                body(i)
            with eng.Fori(1, n // 4 - 1) as j:
                for u in range(4):
                    body(4 * j + u, u)
            for i in range(n - 4, n):
                body(i)

        def entry(engine, q, i, top):
            return nc.values_load(table[0:1, q, bass.ds(i, 1)], engines=(engine,), min_val=0, max_val=top,
                                  skip_runtime_bounds_check_because="the table is computed within these bounds")

        def load_chunk(eng, c):
            eng.dma_start(w_patch[:, c, :], wt[:, c, :]).then_inc(chunk[c], 16)
            eng.dma_start(patches[:, 0, c, :], pt[:, c, 0:BT]).then_inc(chunk[c], 16)

        EMBED_BANK = [0, 1, 2, 3]
        EMBED_BANK_LATER = [6, 7, 6, 7]

        @block.sync
        def _(sp):
            def load_patches(b):
                n = sum(TILES[t] for t in BLOCKS[b])
                sp.dma_start(patches[:, b % 2, :, 0:n], pt[:, :, b * BT:b * BT + n]).then_inc(ld[f"patch{b}"], 16)

            for c in range(0, PC, 2):
                load_chunk(sp, c)
            for dst, src in ((posb, posr), (brow_sb, brow)):
                sp.dma_start(dst[:, :], src).then_inc(ld["first"], 16)
            for dst, src in ((ident, ident_c), (small, small_c)):
                sp.dma_start(dst[:, :], src).then_inc(ld["consts"], 16)
            sp.dma_start(w_qkv[:, :, :], wqkv).then_inc(ld["consts"], 16)
            sp.dma_start(cossin[:, :, :], cs_c).then_inc(ld["consts"], 16)
            for dst, src in ((causal, cmask_c), (hmask, hmask_c), (before, before_c), (w_g2, wg2), (bias_rt, gbias),
                             (w_sd, sd)):
                sp.dma_start(dst[:, :], src).then_inc(ld["rest"], 16)
            for dst, src in ((w_o, wo), (w_g1, wg1), (ln_wb, lnwb), (w_route, gwt), (w_sgu, sgu)):
                sp.dma_start(dst[:, :, :], src).then_inc(ld["rest"], 16)
            load_patches(1)
            sp.wait_ge(ini, 4)
            sp.dma_start(rows_d[0:DUMMY_ROW, :].rearrange("(l r) n -> r l n", r=LIST_ROWS)[0:P, :, :],
                         padrow[:, :].unsqueeze(1).to_broadcast([P, LISTS, ROW])).then_inc(empty, 16)
            sp.dma_start(W[:, 0:LATE[0] * WX], wx[:, 0:LATE[0] * WX]).then_inc(ld["lists"], 16)
            for c in range(CH):
                sp.dma_start(sums_d[c].rearrange("(a p) n -> p a n", p=P),
                             padrow[:, 0:D].unsqueeze(1).to_broadcast([P, SUM_ROWS // P, D])).then_inc(ini_d, 16)
            sp.dma_start(rows_d[DUMMY_ROW:DUMMY_ROW + P, :], padrow[:, :]).then_inc(ini_d, 16)
            sp.wait_ge(emb_ps, len(BLOCKS[0]))
            load_patches(2)

            def load_late(part):
                lo, hi = LATE[part] * WX, LATE[part + 1] * WX
                sp.dma_start(W[:, lo:hi], wx[:, lo:hi]).then_inc(ld[f"late{part}"], 16)

            sp.wait_ge(h_emb, NT)
            load_late(0)
            sp.wait_ge(og_ok, NT)
            load_late(1)
            sp.wait_ge(slot_ok, NT)
            load_late(2)
            sp.wait_ge(scat, 16 * NT * CHOICES)
            sp.wait_ge(ini_d, 16 * (CH + 1))
            sp.wait_ge(table_ok, 1)

            def load_rows(i, u=None):
                u = i if u is None else u
                if not isinstance(i, int) or i >= 4:
                    sp.wait_ge(T_ps, i - 3)
                    sp.wait_ge(meta_ok, i - 3)
                else:
                    sp.wait_ge(en_ok, 4 * NT)
                row = entry(mybir.EngineType.SP, 1, i, DUMMY_ROW)
                sp.dma_start(G[:, u % 4, :], rows_d[bass.ds(row, P), :]).then_inc(g_ld[u % 4], 16)

            groups(sp, load_rows, XT)
            for c in range(CH):
                if c == 0:
                    sp.wait_ge(D_ps, XT)
                sp.wait_ge(added[c], 16 * (XT // CH))
                sp.dma_start(sums[:, c, :, :], sums_d[c][0:FILL_ROW, :].rearrange("(t p) n -> p t n", p=TP)).then_inc(fin_ld[c], 16)
            out_v = out.rearrange("(t p) n -> p t n", p=TP)
            sp.wait_ge(fin_ok, 1)
            sp.dma_start(out_v[:, 0:FIN_DVE, :], h[0:TP, 0:FIN_DVE, :]).then_inc(out_st, 16)
            sp.wait_ge(fin_pool, CH)
            sp.dma_start(out_v[:, FIN_DVE:NT, :], h[0:TP, FIN_DVE:NT, :]).then_inc(out_st, 16)
            sp.wait_ge(out_st, 32)

        @block.gpsimd
        def _(pool):
            pool.memset(ones[:, :], 1.0).then_inc(ini, 1)
            pool.memset(padrow[:, 0:ROW - 1], 0.0)
            pool.iota(padrow_i[:, ROW - 1:ROW], pattern=[[0, 1]], base=FILL_ROW, channel_multiplier=1).then_inc(ini, 1)
            pool.memset(xrow[:, :, D + EXPERTS:D + LISTS], ANCHOR_ALPHA)
            pool.iota(xrow_i[:, :, ROW - 1], pattern=[[TP, NT]], base=0, channel_multiplier=1).then_inc(ini, 1)
            pool.memset(h[:, :, :], 0.0).then_inc(ini, 1)
            pool.wait_ge(ini, 4)
            pool.wait_ge(ld["rest"], 16 * 11)

            def split_heads(t):
                n = TILES[t]
                pool.wait_ge(qkT_ok, t + 1)
                if t >= 2:
                    pool.wait_ge(en_ps, 4 * (t - 1))
                for k in range(KC):
                    pool.tensor_tensor(q_heads[:, t % 2, 8 * k:8 * k + 8, 0:n],
                                       qT[:, t % 2, k, 0:n].unsqueeze(1).to_broadcast([P, 8, n]),
                                       hmask[:, :].unsqueeze(2).to_broadcast([P, 8, n]), ALU.mult).then_inc(qh_ok, 1)

            def scatter(t):
                n = TILES[t]
                pool.wait_ge(slot_ok, t + 1)
                if t == 0:
                    pool.wait_ge(empty, 16)
                for j in range(CHOICES):
                    pool.indirect_dma_start(rows_d, bass.IndirectOffsetOnAxis(ap=slot[0:n, t, j:j + 1], axis=0),
                                            xrow[0:n, t, :], None).then_inc(scat, 16)

            for b, tiles in enumerate(BLOCKS):
                for t in tiles:
                    split_heads(t)
                if b:
                    for t in BLOCKS[b - 1]:
                        scatter(t)
            for t in BLOCKS[-1]:
                scatter(t)

            def add_rows(i, u=None):
                c = i % CH if u is None else u
                pool.wait_ge(Y_ok, i + 1)
                if not isinstance(i, int) or i >= CH:
                    pool.wait_ge(added[c], (i - c) * (16 // CH))
                pool.nop(nofuse=True)
                pool.tensor_copy(tok[:, c:c + 1], tok_of[:, bass.ds(i, 1)]).then_inc(tok_ok, 1)
                pool.wait_ge(tok_ok, i + 1)
                pool.nop(nofuse=True)
                pool.indirect_dma_start(sums_d[c], bass.IndirectOffsetOnAxis(ap=tok[:, c:c + 1], axis=0),
                                        Y[:, c, :], None, compute_op=ALU.add).then_inc(added[c], 16)

            groups(pool, add_rows, XT)
            for c in range(CH):
                pool.wait_ge(fin_ld[c], 16)
                if c:
                    pool.wait_ge(fin_pool, c)
                pool.tensor_tensor(h[0:TP, FIN_DVE:NT, :], h[0:TP, FIN_DVE:NT, :], sums[:, c, FIN_DVE:NT, :],
                                   ALU.add).then_inc(fin_pool, 1)

        @block.tensor
        def _(pe):
            def out_project(t):
                n = TILES[t]
                pe.wait_ge(ynT_ok, t + 1)
                if t >= 2:
                    pe.wait_ge(h2_ok, t - 1)
                for k in range(KC):
                    m = pe.matmul(B[4 + t % 2][0:n, 0:D], ynT[:, t % 2, k, 0:n], w_o[:, k, :],
                                  start=k == 0, stop=k == KC - 1)
                m.then_inc(wo_ps, 1)

            def route(t):
                n, r = TILES[t], t * TT
                pe.wait_ge(x2T_ok, t + 1)
                if t >= 2:
                    pe.wait_ge(rt_ok, t - 1)
                for k in range(KC):
                    m = pe.matmul(B[t % 2][0:n, 0:EXPERTS], x2T[:, k, r:r + n], w_route[:, k, :],
                                  start=k == 0, stop=k == KC - 1)
                m.then_inc(rt_ps, 1)

            def rank(t):
                n, at = TILES[t], t % 4 * P
                pe.wait_ge(ch_ok, t + 1)
                pe.matmul(B[7][0:n, at:at + LISTS], before[0:n, 0:n], chosen[0:n, t % 4, :], start=True, stop=True)
                pe.matmul(B[7][:, at + LISTS:at + 2 * LISTS], ones[0:n, :], chosen[0:n, t % 4, :],
                          start=True, stop=True).then_inc(rank_ps, 1)

            def embed(t, bank):
                n, b = TILES[t], t // 4
                pe.wait_ge(ld[f"patch{b}"], 16)
                for c in range(PC):
                    m = pe.matmul(B[bank][0:n, 0:D], patches[:, b % 2, c, cols(t):cols(t) + n], w_patch[:, c, :],
                                  start=c == 0, stop=c == PC - 1)
                m.then_inc(emb_ps, 1)

            def transpose2(bank, src, n, done):
                for k in range(KC):
                    m = pe.transpose(bank[:, k * TT:k * TT + n], src[0:n, k * P:(k + 1) * P], ident[0:n, 0:n])
                m.then_inc(done, 1)

            def project(t):
                n = TILES[t]
                for ps, lo, hi, done in ((B[4 + t % 2], 0, 2 * D, qk_ps), (B[6 + t % 2], 2 * D, 3 * D, v_ps)):
                    for k in range(KC):
                        m = pe.matmul(ps[0:n, 0:hi - lo], xnT[:, k, cols(t):cols(t) + n], w_qkv[:, k, lo:hi],
                                      start=k == 0, stop=k == KC - 1)
                    m.then_inc(done, 1)
                if t >= 2:
                    pe.wait_ge(gate_ok, t - 1)
                for k in range(KC):
                    m = pe.matmul(B[t % 2][0:HD, D:D + n], w_g1[:, k, :], xnT[:, k, cols(t):cols(t) + n],
                                  start=k == 0, stop=k == KC - 1)
                m.then_inc(g1_ps, 1)

            def gate(t):
                n = TILES[t]
                pe.wait_ge(g1_ok, t + 1)
                if t >= 2:
                    pe.wait_ge(gate_ok, t - 1)
                pe.matmul(B[t % 2][0:n, 0:D], g1T[:, t % 2, 0:n], w_g2[:, :], start=True, stop=True).then_inc(gate_ps, 1)

            def qk_transpose(t):
                n = TILES[t]
                pe.wait_ge(rope_ok, t + 1)
                if t >= 2:
                    pe.wait_ge(qkT_ok, t - 1)
                for k in range(2 * KC):
                    m = pe.transpose(B[2 + t % 2][:, k * TT:k * TT + n], qk[0:n, t % 4, k * P:(k + 1) * P],
                                     ident[0:n, 0:n])
                m.then_inc(qkT_ps, 1)

            def energies(t):
                n = TILES[t]
                for g in range(4):
                    i = 4 * t + g
                    if g % 2 == 0:
                        pe.wait_ge(qh_ok, 2 * t + g // 2 + 1)
                    if i >= 3:
                        pe.wait_ge(en_ok, i - 2)
                    pe.matmul(B[4 + i % 3][0:n, 0:4 * n], kT[:, t % 2, g // 2, 0:n],
                              q_heads[:, t % 2, 4 * g:4 * g + 4, 0:n],
                              start=True, stop=True).then_inc(en_ps, 1)

            def attend(t):
                n = TILES[t]
                pe.wait_ge(en_ok, 4 * t + 4)
                if t >= 2:
                    pe.wait_ge(og_ok, t - 1)
                for hd in range(HEADS):
                    m = pe.matmul(B[t % 2][0:n, hd * HD:(hd + 1) * HD], energy[0:n, t % 2, hd, 0:n],
                                  v_sb[0:n, t % 4, hd * HD:(hd + 1) * HD], start=True, stop=True)
                m.then_inc(av_ps, 1)

            for c in range(PC):
                pe.wait_ge(chunk[c], 32)
                for t in BLOCKS[0]:
                    m = pe.matmul(B[EMBED_BANK[t]][0:TILES[t], 0:D], patches[:, 0, c, cols(t):cols(t) + TILES[t]],
                                  w_patch[:, c, :], start=c == 0, stop=c == PC - 1)
                    if c == PC - 1:
                        m.then_inc(emb_ps, 1)
            pe.wait_ge(ld["consts"], 16 * 4)
            pe.wait_ge(ini, 4)
            for b, tiles in enumerate(BLOCKS):
                t0, t1 = tiles[0], tiles[-1] + 1
                for t in tiles:
                    pe.wait_ge(xn_ok, t + 1)
                    if t >= 2:
                        pe.wait_ge(xnT_ok, t - 1)
                    transpose2(B[2 + t % 2], xn[:, t % 4, :], TILES[t], xnT_ps)
                if b == 0:
                    pe.wait_ge(ld["rest"], 16 * 11)
                else:
                    pe.wait_ge(rt_ok, t0)
                for t in tiles:
                    pe.wait_ge(xnT_ok, t + 1)
                    if t >= 2:
                        pe.wait_ge(qk_ok, t - 1)
                        pe.wait_ge(v_ok, t - 1)
                        pe.wait_ge(g1_ok, t - 1)
                    project(t)
                    if t > t0:
                        gate(t - 1)
                    if t == t0 + 2:
                        qk_transpose(t0)
                gate(t1 - 1)
                qk_transpose(t0 + 1)
                if b:
                    pe.wait_ge(v_ok, t1)
                    for t in BLOCKS[b - 1]:
                        rank(t)
                pe.wait_ge(qk_ok, t1)
                pe.wait_ge(v_ok, t1)
                for t in tiles:
                    if t > t0 and t + 1 < t1:
                        qk_transpose(t + 1)
                    energies(t)
                    if t == t0:
                        pe.wait_ge(gate_ok, t1)
                    if t > t0:
                        attend(t - 1)
                attend(t1 - 1)
                following = BLOCKS[b + 1] if b + 1 < len(BLOCKS) else []
                if b:
                    pe.wait_ge(slot_ok, t0)
                for t in following[:2]:
                    embed(t, EMBED_BANK_LATER[t % 4])
                for t in tiles:
                    pe.wait_ge(yn_ok, t + 1)
                    if t >= 2:
                        pe.wait_ge(ynT_ok, t - 1)
                    transpose2(B[2 + t % 2], xn[:, t % 4, :], TILES[t], ynT_ps)
                    if t > t0:
                        out_project(t - 1)
                out_project(t1 - 1)
                for t in following[2:]:
                    pe.wait_ge(h_emb, t - 1)
                    embed(t, EMBED_BANK_LATER[t % 4])
                for t in tiles:
                    pe.wait_ge(x2_ok, t + 1)
                    if t >= 2:
                        pe.wait_ge(x2T_ok, t - 1)
                    transpose2(B[2 + t % 2], xrow[:, t, :], TILES[t], x2T_ps)
                    if t > t0:
                        route(t - 1)
                route(t1 - 1)

            def s_up(t):
                n, r = TILES[t], t * TT
                if t >= 2:
                    pe.wait_ge(sh_ok, t - 1)
                for k in range(KC):
                    m = pe.matmul(B[4 + t % 2][0:n, 0:D], x2T[:, k, r:r + n], w_sgu[:, k, :],
                                  start=k == 0, stop=k == KC - 1)
                m.then_inc(sgu_ps, 1)

            def s_transpose(t):
                n = TILES[t]
                pe.wait_ge(sh_ok, t + 1)
                if t >= 2:
                    pe.wait_ge(shT_ok, t - 1)
                pe.transpose(B[2 + t % 2][:, 0:n], H[0:n, t % 2, :], ident[0:n, 0:n]).then_inc(shT_ps, 1)

            def s_down(t):
                n = TILES[t]
                pe.wait_ge(shT_ok, t + 1)
                if t >= 2:
                    pe.wait_ge(hs_ok, t - 1)
                pe.matmul(B[t % 2][0:n, 0:D], HT[:, t % 2, 0:n], w_sd[:, :],
                          start=True, stop=True).then_inc(sd_ps, 1)

            pe.wait_ge(h2_ok, NT)
            pe.wait_ge(rt_ok, NT)
            s_up(0)
            s_up(1)
            for t in BLOCKS[-1]:
                rank(t)
            for t in range(NT):
                if t >= 2:
                    s_up(t)
                if t >= 1:
                    s_transpose(t - 1)
                if t >= 2:
                    s_down(t - 2)
            s_transpose(NT - 1)
            s_down(NT - 2)
            s_down(NT - 1)
            pe.wait_ge(cols_ok, 1)
            for q in range(3):
                pe.matmul(B[6][0:1, q * P:(q + 1) * P], tcol[:, q:q + 1], ident[:, :], start=True, stop=True)
            pe.matmul(B[6][:, 3 * P:4 * P], ones[:, :], dups[:, :], start=True, stop=True).then_inc(table_ps, 1)

            pe.wait_ge(ld["lists"], 16)
            for part in range(3):
                pe.wait_ge(ld[f"late{part}"], 16)
            pe.wait_ge(table_ok, 1)
            pe.wait_ge(hs_ok, NT)
            pe.wait_ge(shT_ok, NT)

            def turn_rows(i, u):
                if not isinstance(i, int) or i >= 2:
                    pe.wait_ge(gt_ok, i - 1)
                pe.wait_ge(g_ld[u % 4], (i - u % 4) * 4 + 16)
                for k in range(KC):
                    m = pe.transpose(B[u % 2][:, k * P:(k + 1) * P], G[:, u % 4, k * P:(k + 1) * P], ident[:, :])
                m.then_inc(T_ps, 1)

            def up(i, u, e):
                pe.wait_ge(gt_ok, i + 1)
                for k in range(KC):
                    m = pe.matmul(B[2 + u % 2][:, 0:D], GT[:, u % 2, k, :], W[:, bass.ds(e, WX)][:, k * D:(k + 1) * D],
                                  start=k == 0, stop=k == KC - 1)
                m.then_inc(U_ps, 1)

            def turn_hidden(i, u):
                pe.wait_ge(H_ok, i + 1)
                pe.transpose(B[4 + u % 2][:, 0:P], H[:, u % 2, :], ident[:, :]).then_inc(HT_ps, 1)

            def down(i, u, e):
                pe.wait_ge(HT_ok, i + 1)
                if not isinstance(i, int) or i >= 2:
                    pe.wait_ge(Y_ok, i - 1)
                pe.matmul(B[6 + u % 2][:, 0:D], HT[:, u % 2, :], W[:, bass.ds(e, WX)][:, KC * D:(KC + 1) * D],
                          start=True, stop=True).then_inc(D_ps, 1)

            held = {}

            def weights_of(i, u):
                if u not in held:
                    held[u] = entry(mybir.EngineType.PE, 0, i, (LISTS - 1) * WX)
                return held[u]

            def list_tile(i, u=None):
                if u in (None, 0):
                    held.clear()
                u = i if u is None else u + 4
                up(i, u, weights_of(i, u))
                if not isinstance(i, int) or i >= 1:
                    turn_hidden(i - 1, u - 1)
                if not isinstance(i, int) or i >= 2:
                    down(i - 2, u - 2, weights_of(i - 2, u - 2))
                if not isinstance(i, int) or i + 2 < XT:
                    turn_rows(i + 2, u + 2)

            turn_rows(0, 0)
            turn_rows(1, 1)
            groups(pe, list_tile, XT)
            held.clear()
            turn_hidden(XT - 1, XT - 1)
            down(XT - 2, XT - 2, weights_of(XT - 2, XT - 2))
            down(XT - 1, XT - 1, weights_of(XT - 1, XT - 1))

        @block.scalar
        def _(act):
            for c in range(1, PC, 2):
                load_chunk(act, c)

            def gate_tanh(t):
                n = TILES[t]
                act.wait_ge(gate_ps, t + 1)
                act.activation(gate_th[0:n, t % 4, :], B[t % 2][0:n, 0:D], ACT.Tanh, scale=0.5).then_inc(gate_ok, 1)

            def copy2(dst, bank, n, s, v, done):
                act.wait_ge(s, v)
                act.copy(dst, bank[:, 0:KC * TT].rearrange("p (k t) -> p k t", k=KC)[:, :, 0:n]).then_inc(done, 1)

            def normal(dst, src, t, done):
                n = TILES[t]
                act.activation(dst, src, ACT.Identity, scale=nwt[0:n, 1, t % 4:t % 4 + 1],
                               bias=nwt[0:n, 3, t % 4:t % 4 + 1]).then_inc(done, 1)

            def qk_copy(t):
                n = TILES[t]
                act.wait_ge(qkT_ps, t + 1)
                if t >= 2:
                    act.wait_ge(en_ps, 4 * (t - 1))
                act.copy(qT[:, t % 2, :, 0:n], B[2 + t % 2][:, 0:KC * TT]
                         .rearrange("p (k t) -> p k t", k=KC)[:, :, 0:n])
                act.copy(kT[:, t % 2, :, 0:n], B[2 + t % 2][:, KC * TT:2 * KC * TT]
                         .rearrange("p (k t) -> p k t", k=KC)[:, :, 0:n]).then_inc(qkT_ok, 1)

            for b, tiles in enumerate(BLOCKS):
                t0, t1 = tiles[0], tiles[-1] + 1

                def x_copy(t):
                    copy2(xnT[:, :, cols(t):cols(t) + TILES[t]], B[2 + t % 2], TILES[t], xnT_ps, t + 1, xnT_ok)

                act.wait_ge(ln_ok, 3 * b + 1)
                if b:
                    act.wait_ge(ynT_ps, t0)
                for t in tiles:
                    normal(xn[0:TILES[t], t % 4, :], h[0:TILES[t], t, :], t, xn_ok)
                    if t > t0:
                        x_copy(t - 1)
                x_copy(t1 - 1)
                for t in tiles:
                    n = TILES[t]
                    act.wait_ge(qk_ps, t + 1)
                    act.activation(qk[0:n, t % 4, :], B[4 + t % 2][0:n, :], ACT.Silu).then_inc(qk_ok, 1)
                    act.wait_ge(v_ps, t + 1)
                    act.copy(v_sb[0:n, t % 4, :], B[6 + t % 2][0:n, 0:D]).then_inc(v_ok, 1)
                    act.wait_ge(g1_ps, t + 1)
                    if t >= 2:
                        act.wait_ge(gate_ps, t - 1)
                    act.copy(g1T[:, t % 2, 0:n], B[t % 2][0:HD, D:D + n]).then_inc(g1_ok, 1)
                    if t > t0:
                        gate_tanh(t - 1)
                    if t == t0 + 2:
                        qk_copy(t0)
                gate_tanh(t1 - 1)
                for t in tiles[1:]:
                    qk_copy(t)

                def yn_copy(t):
                    n = TILES[t]
                    act.wait_ge(ynT_ps, t + 1)
                    if t >= 2:
                        act.wait_ge(wo_ps, t - 1)
                    for k in range(KC):
                        m = act.activation(ynT[:, t % 2, k, 0:n], B[2 + t % 2][:, k * TT:k * TT + n], ACT.Identity,
                                           scale=ln_wb[:, k, 0:1], bias=ln_wb[:, k, 1:2])
                    m.then_inc(ynT_ok, 1)

                act.wait_ge(ln_ok, 3 * b + 2)
                for t in tiles:
                    normal(xn[0:TILES[t], t % 4, :], xn[0:TILES[t], t % 4, :], t, yn_ok)
                    if t > t0:
                        yn_copy(t - 1)
                yn_copy(t1 - 1)

                def x2_copy(t):
                    n, r = TILES[t], t * TT
                    copy2(x2T[:, :, r:r + n], B[2 + t % 2], n, x2T_ps, t + 1, x2T_ok)

                act.wait_ge(ln_ok, 3 * b + 3)
                for t in tiles:
                    normal(xrow[0:TILES[t], t, 0:D], h[0:TILES[t], t, :], t, x2_ok)
                    if t > t0:
                        x2_copy(t - 1)
                x2_copy(t1 - 1)
                for t in tiles:
                    n = TILES[t]
                    act.wait_ge(rt_ps, t + 1)
                    if b:
                        act.wait_ge(ch_done, b)
                    act.activation(sig[0:n, t % 4, :], B[t % 2][0:n, 0:EXPERTS], ACT.Sigmoid).then_inc(rt_ok, 1)
            def s_silu(t):
                n = TILES[t]
                act.wait_ge(sgu_ps, t + 1)
                if t >= 2:
                    act.wait_ge(sh_ok, t - 1)
                act.activation(S[0:n, t % 2, :], B[4 + t % 2][0:n, 0:P], ACT.Silu).then_inc(ssilu_ok, 1)

            def s_copy(t):
                n = TILES[t]
                act.wait_ge(shT_ps, t + 1)
                if t >= 2:
                    act.wait_ge(sd_ps, t - 1)
                act.copy(HT[:, t % 2, 0:n], B[2 + t % 2][:, 0:n]).then_inc(shT_ok, 1)

            s_silu(0)
            s_silu(1)
            for t in range(NT):
                if t >= 2:
                    s_silu(t)
                if t >= 1:
                    s_copy(t - 1)
            s_copy(NT - 1)

            def hidden_silu(i, u=None):
                v = i if u is None else u
                act.wait_ge(U_ps, i + 1)
                if not isinstance(i, int) or i >= 2:
                    act.wait_ge(H_ok, i - 1)
                act.activation(S[:, v % 2, :], B[2 + v % 2][:, 0:P], ACT.Silu).then_inc(silu_ok, 1)
                if not isinstance(i, int) or i >= 2:
                    weigh(i - 2, v + 2)

            def weigh(i, v):
                act.wait_ge(D_ps, i + 1)
                act.wait_ge(meta_ok, i + 1)
                if not isinstance(i, int) or i >= CH:
                    act.wait_ge(added[v % 4], (i - v % 4) * (16 // CH))
                act.activation(Y[:, v % 4, :], B[6 + v % 2][:, 0:D], ACT.Copy, scale=wcol[:, bass.ds(i, 1)]).then_inc(Y_ok, 1)

            groups(act, hidden_silu, XT)
            weigh(XT - 2, XT - 2)
            weigh(XT - 1, XT - 1)

        @block.vector
        def _(dve):
            count, norms = [0], [0]

            def step(ins):
                count[0] += 1
                ins.then_inc(dchain, 1)
                dve.wait_ge(dchain, count[0])

            def stat(src, t):
                n = TILES[t]
                step(dve.bn_stats(stats[0:n, t % 4, :], src))
                step(dve.bn_aggr(mv[0:n, t % 4, :], stats[0:n, t % 4, :]))

            def deviations(k, eps):
                v, y, a = nwt[:, 0, 0:k], nwt[:, 1, 0:k], nwt[:, 2, 0:k]
                vi, yi, ai_ = nwt_i[:, 0, 0:k], nwt_i[:, 1, 0:k], nwt_i[:, 2, 0:k]
                step(dve.tensor_scalar(v, mv[:, 0:k, 1], eps, None, ALU.add))
                step(dve.tensor_scalar(ai_, vi, 1, None, ALU.logical_shift_right))
                step(dve.tensor_scalar(yi, ai_, -1.0, float(0x5F3759DF), ALU.mult, ALU.add))
                for _ in range(3):
                    step(dve.scalar_tensor_tensor(a, y, -0.5, y, ALU.mult, ALU.mult))
                    step(dve.tensor_tensor(a, a, v, ALU.mult))
                    step(dve.scalar_tensor_tensor(y, a, 1.5, y, ALU.add, ALU.mult))
                norms[0] += 1
                dve.scalar_tensor_tensor(nwt[:, 3, 0:k], mv[:, 0:k, 0], -1.0, y, ALU.mult, ALU.mult).then_inc(ln_ok, 1)
                dve.wait_ge(ln_ok, norms[0])

            def choose(b):
                t0, k, n = BLOCKS[b][0], len(BLOCKS[b]), TT
                t1 = t0 + k
                s, sct = sig[0:n, 0:k, :], sc[0:n, 0:k, :]
                g0, g1, g2, g3 = (gs[0:n, q, 0:GROUPS * k] for q in range(4))
                by_group = sct.rearrange("p k (g e) -> p (k g) e", g=GROUPS)
                pair = [n, k, GROUPS, GROUPS]
                g0_t = g0.rearrange("p (k g) -> p k g", k=k)
                ahead, tie = cmp[0:n, 0, 0:k], cmp[0:n, 1, 0:k]

                dve.wait_ge(rt_ok, t1)
                if t0:
                    dve.wait_ge(rank_ps, t0)
                step(dve.tensor_tensor(sct, s, bias_rt[0:n, :].unsqueeze(1).to_broadcast([n, k, EXPERTS]), ALU.add))
                for g in range(GROUPS * k):
                    m = dve.max(top8[0:n, g, :], by_group[:, g, :])
                step(m)
                step(dve.tensor_tensor(g0, top8[0:n, 0:GROUPS * k, 0], top8[0:n, 0:GROUPS * k, 1], ALU.add))
                others, own = g0_t.unsqueeze(2).to_broadcast(pair), g0_t.unsqueeze(3).to_broadcast(pair)
                dve.tensor_tensor(ahead, others, own, ALU.is_gt)
                step(dve.tensor_tensor(tie, others, own, ALU.is_equal))
                step(dve.tensor_tensor(tie, tie, tri4[0:n, :].rearrange("p (a b) -> p a b", a=GROUPS)
                                       .unsqueeze(1).to_broadcast(pair), ALU.mult))
                step(dve.tensor_tensor(ahead, ahead, tie, ALU.add))
                step(dve.reduce_sum(g1.rearrange("p (k g) -> p k g", k=k), ahead, axis=AX.X))
                step(dve.tensor_scalar(g2, g1, 2.0, None, ALU.is_lt))
                step(dve.tensor_scalar(g3, g2, BIG, -BIG, ALU.mult, ALU.add))
                step(dve.tensor_tensor(by_group, by_group, g2.unsqueeze(2).to_broadcast([n, GROUPS * k, GE]), ALU.mult))
                step(dve.tensor_tensor(by_group, by_group, g3.unsqueeze(2).to_broadcast([n, GROUPS * k, GE]), ALU.add))
                for u in range(k):
                    m = dve.max(tv[0:n, u, :], sc[0:n, u, :])
                step(m)
                for u in range(k):
                    m = dve.max_index(ti[0:n, u, :], tv[0:n, u, :], sc[0:n, u, :])
                step(m)
                dve.tensor_copy(idx[0:n, 0:k, 0:TOPK], ti[0:n, 0:k, 0:TOPK])
                step(dve.tensor_scalar(ai[0:n, 0:k], ti[0:n, 0:k, 0], 1, None, ALU.logical_shift_right))
                step(dve.tensor_scalar(idx[0:n, 0:k, TOPK], ai[0:n, 0:k], float(EXPERTS), None, ALU.add))
                for u in range(k):
                    m = dve.tensor_tensor(oh[0:n, u], idx[0:n, u, :].unsqueeze(2).to_broadcast([n, CHOICES, LISTS]),
                                          iota_l[0:n, :].unsqueeze(1).to_broadcast([n, CHOICES, LISTS]), ALU.is_equal)
                step(m)
                for u in range(k):
                    dve.reduce_sum(chosen[0:n, u, :], oh[0:n, u].rearrange("p j e -> p e j"), axis=AX.X).then_inc(ch_ok, 1)
                dve.wait_ge(ch_ok, t1)
                w = xrow[0:n, t0:t1, D:D + EXPERTS]
                step(dve.tensor_tensor(w, chosen[0:n, 0:k, 0:EXPERTS], s, ALU.mult))
                step(dve.reduce_sum(wsum[0:n, 0, 0:k], w, axis=AX.X))
                step(dve.tensor_scalar(wsum[0:n, 0, 0:k], wsum[0:n, 0, 0:k], 1e-20, None, ALU.add))
                step(dve.reciprocal(wsum[0:n, 1, 0:k], wsum[0:n, 0, 0:k]))
                step(dve.tensor_scalar(wsum[0:n, 1, 0:k], wsum[0:n, 1, 0:k], ROUTED_SCALE, None, ALU.mult))
                dve.tensor_tensor(w, w, wsum[0:n, 1, 0:k].unsqueeze(2).to_broadcast([n, k, EXPERTS]),
                                  ALU.mult).then_inc(ch_done, 1)
                dve.wait_ge(ch_done, b + 1)

            def place(t, t1):
                n, at = TILES[t], t % 4 * P
                dve.wait_ge(rank_ps, t1)
                step(dve.tensor_tensor(rnk[0:n, :], B[7][0:n, at:at + LISTS], base[0:n, :], ALU.add))
                dve.tensor_tensor(base[:, :], base[:, :], B[7][:, at + LISTS:at + 2 * LISTS], ALU.add)
                step(dve.tensor_tensor(prod[0:n], oh[0:n, t % 4], rnk[0:n, :].unsqueeze(1).to_broadcast([n, CHOICES, LISTS]),
                                       ALU.mult))
                step(dve.reduce_sum(slot_f[0:n, :], prod[0:n], axis=AX.X))
                dve.tensor_copy(slot[0:n, t, :], slot_f[0:n, :]).then_inc(slot_ok, 1)
                dve.wait_ge(slot_ok, t + 1)

            def embedded(t, bank):
                n = TILES[t]
                dve.wait_ge(emb_ps, t + 1)
                dve.tensor_tensor(h[0:n, t, :], B[bank][0:n, 0:D], posb[0:n, :], ALU.add).then_inc(h_emb, 1)
                dve.wait_ge(h_emb, t + 1)

            def rope(t):
                n = TILES[t]
                dve.wait_ge(qk_ok, t + 1)
                q = qk[0:n, t % 4, :].rearrange("p (h d) -> p h d", d=HD)
                a = rp[0:n, 0, :].rearrange("p (h d) -> p h d", d=HD)
                r_ = rp[0:n, 1, :].rearrange("p (h d) -> p h d", d=HD)
                half = HD // 2

                def tab(i, lo, hi):
                    return cossin[0:n, i, lo:hi].unsqueeze(1).to_broadcast([n, 2 * HEADS, hi - lo])

                dve.tensor_tensor(a, q, tab(0, 0, HD), ALU.mult)
                dve.tensor_tensor(r_[:, :, 0:half], q[:, :, half:HD], tab(1, 0, half), ALU.mult)
                step(dve.tensor_tensor(r_[:, :, half:HD], q[:, :, 0:half], tab(1, half, HD), ALU.mult))
                dve.tensor_tensor(q, a, r_, ALU.add).then_inc(rope_ok, 1)
                dve.wait_ge(rope_ok, t + 1)

            def mask_energy(t):
                n = TILES[t]
                if t >= 2:
                    dve.wait_ge(av_ps, t - 1)
                for g in range(4):
                    i = 4 * t + g
                    dve.wait_ge(en_ps, i + 1)
                    dve.tensor_tensor(energy[0:n, t % 2, 4 * g:4 * g + 4, 0:n],
                                      B[4 + i % 3][0:n, 0:4 * n].rearrange("p (h t) -> p h t", h=4),
                                      causal[0:n, 0:n].unsqueeze(1).to_broadcast([n, 4, n]),
                                      ALU.mult).then_inc(en_ok, 1)

            def apply_gate(t):
                n = TILES[t]
                dve.wait_ge(av_ps, t + 1)
                dve.wait_ge(gate_ok, t + 1)
                dve.scalar_tensor_tensor(xn[0:n, t % 4, :], gate_th[0:n, t % 4, :], 1.0,
                                         B[t % 2][0:n, 0:D], ALU.add, ALU.mult).then_inc(og_ok, 1)
                dve.wait_ge(og_ok, t + 1)
                stat(xn[0:n, t % 4, :], t)

            step(dve.memset(mv[:, :, :], 1.0))
            dve.wait_ge(ld["first"], 16 * 2)
            dve.wait_ge(ini, 4)
            step(dve.tensor_tensor(posb[:, :], posb[:, :], brow_sb[:, :], ALU.add))
            for t in BLOCKS[0]:
                embedded(t, EMBED_BANK[t % 4])
                stat(h[0:TILES[t], t, :], t)
            deviations(len(BLOCKS[0]), EPS)
            dve.wait_ge(ld["consts"], 16 * 4)
            step(dve.tensor_copy(base[:, :], base0))
            dve.wait_ge(ld["rest"], 16 * 11)
            for b, tiles in enumerate(BLOCKS):
                t0, t1 = tiles[0], tiles[-1] + 1
                if b:
                    choose(b - 1)
                for t in tiles:
                    rope(t)
                before_this = list(BLOCKS[b - 1]) if b else []
                for t in tiles:
                    mask_energy(t)
                    if t > t0:
                        apply_gate(t - 1)
                    if before_this:
                        place(before_this.pop(0), t0)
                for t in before_this:
                    place(t, t0)
                apply_gate(t1 - 1)
                dve.wait_ge(xn_ok, t1)
                deviations(len(tiles), 4 * EPS)
                following = BLOCKS[b + 1] if b + 1 < len(BLOCKS) else []
                for t in following[:2]:
                    embedded(t, EMBED_BANK_LATER[t % 4])
                for t in tiles:
                    n = TILES[t]
                    dve.wait_ge(wo_ps, t + 1)
                    dve.tensor_tensor(h[0:n, t, :], B[4 + t % 2][0:n, 0:D], h[0:n, t, :], ALU.add).then_inc(h2_ok, 1)
                    dve.wait_ge(h2_ok, t + 1)
                    stat(h[0:n, t, :], t)
                dve.wait_ge(yn_ok, t1)
                deviations(len(tiles), EPS)
                for t in following[2:]:
                    embedded(t, EMBED_BANK_LATER[t % 4])
                if following:
                    for t in following:
                        stat(h[0:TILES[t], t, :], t)
                    dve.wait_ge(x2_ok, t1)
                    deviations(len(following), EPS)

            def s_mult(t):
                n = TILES[t]
                dve.wait_ge(ssilu_ok, t + 1)
                if t >= 2:
                    dve.wait_ge(shT_ps, t - 1)
                dve.tensor_tensor(H[0:n, t % 2, :], S[0:n, t % 2, :], B[4 + t % 2][0:n, P:2 * P],
                                  ALU.mult).then_inc(sh_ok, 1)

            def s_add(t):
                n = TILES[t]
                dve.wait_ge(sd_ps, t + 1)
                dve.tensor_tensor(h[0:n, t, :], B[t % 2][0:n, 0:D], h[0:n, t, :], ALU.add).then_inc(hs_ok, 1)

            choose(len(BLOCKS) - 1)
            s_mult(0)
            s_mult(1)
            for t in BLOCKS[-1]:
                place(t, NT)
            counts, tiles_of, ends, starts, mine, t5 = (tabf[:, q, :] for q in range(6))
            list_c, row_c, weight_c, start_c, over_c, base_c, used_c, dup_c = (tcol[:, q:q + 1] for q in range(8))
            step(dve.tensor_tensor(counts, base[:, :], base0, ALU.subtract))
            step(dve.tensor_scalar(cnt_i[:, :], counts, float(P - 1), None, ALU.add))
            step(dve.tensor_scalar(cnt_i[:, :], cnt_i[:, :], 7, None, ALU.logical_shift_right))
            step(dve.tensor_copy(tiles_of, cnt_i[:, :]))
            dve.tensor_tensor_scan(ends[:, 0:EXPERTS], ones[:, 0:EXPERTS], tiles_of[:, 0:EXPERTS], 0.0, ALU.mult, ALU.add)
            step(dve.tensor_tensor_scan(ends[:, EXPERTS:LISTS], ones[:, 0:ANCHORS], tiles_of[:, EXPERTS:LISTS],
                                        float(ROUTED_TILES), ALU.mult, ALU.add))
            step(dve.tensor_tensor(starts, ends, tiles_of, ALU.subtract))
            dve.tensor_scalar(mine, starts, pcol, None, ALU.is_le)
            step(dve.tensor_scalar(t5, ends, pcol, None, ALU.is_gt))
            step(dve.tensor_tensor(mine, mine, t5, ALU.mult))
            step(dve.tensor_scalar(counts, counts, -float(P), 0.0, ALU.add, ALU.max))
            dve.reduce_sum(used_c, mine, axis=AX.X)
            for col, of_list in ((start_c, starts), (over_c, counts), (base_c, base0), (list_c, iota_l)):
                step(dve.tensor_tensor(t5, mine, of_list, ALU.mult))
                step(dve.reduce_sum(col, t5, axis=AX.X))
            step(dve.tensor_tensor(dup_c, pcol, start_c, ALU.subtract))
            step(dve.tensor_scalar(dup_c, dup_c, float(P), None, ALU.mult))
            step(dve.tensor_tensor(row_c, dup_c, over_c, ALU.min))
            step(dve.tensor_tensor(dup_c, dup_c, row_c, ALU.subtract))
            step(dve.tensor_tensor(row_c, row_c, base_c, ALU.add))
            step(dve.tensor_scalar(used_c, used_c, -float(DUMMY_ROW), float(DUMMY_ROW), ALU.mult, ALU.add))
            dve.tensor_tensor(row_c, row_c, used_c, ALU.add)
            dve.tensor_scalar(dups[:, :], ident[:, :], dup_c, None, ALU.mult)
            dve.tensor_scalar(weight_c, list_c, float(D), None, ALU.add)
            step(dve.tensor_scalar(start_c, list_c, float(WX), None, ALU.mult))
            dve.tensor_copy(list_c, start_c).then_inc(cols_ok, 1)

            for t in range(NT):
                if t >= 2:
                    s_mult(t)
                    s_add(t - 2)
            s_add(NT - 2)
            s_add(NT - 1)
            dve.wait_ge(table_ps, 1)
            dve.tensor_copy(table[:, :, :].rearrange("p a b -> p (a b)"), B[6][0:1, 0:3 * P])
            dve.tensor_scalar(fresh[:, :], B[6][:, 3 * P:4 * P], pcol, None, ALU.is_le).then_inc(table_ok, 1)
            dve.wait_ge(table_ok, 1)

            def take_rows(i, v):
                dyn = not isinstance(i, int)
                dve.wait_ge(T_ps, i + 1)
                if dyn or i >= 2:
                    dve.wait_ge(U_ps, i - 1)
                dve.tensor_copy(GT[:, v % 2, :, :].rearrange("p k s -> p (k s)"), B[v % 2][:, 0:D]).then_inc(gt_ok, 1)
                at = entry(mybir.EngineType.DVE, 2, i, ROW - 1)
                dve.tensor_tensor(wcol[:, bass.ds(i, 1)], G[:, v % 4, bass.ds(at, 1)], fresh[:, bass.ds(i, 1)], ALU.mult)
                dve.tensor_copy(tok_of[:, bass.ds(i, 1)], G_i[:, v % 4, ROW - 1:ROW]).then_inc(meta_ok, 1)

            def hidden_copy(i, v):
                dve.wait_ge(HT_ps, i + 1)
                if not isinstance(i, int) or i >= 2:
                    dve.wait_ge(D_ps, i - 1)
                dve.tensor_copy(HT[:, v % 2, :], B[4 + v % 2][:, 0:P]).then_inc(HT_ok, 1)

            def tile_steps(i, u=None):
                v = i if u is None else u + 4
                dyn = not isinstance(i, int)
                dve.wait_ge(silu_ok, i + 1)
                if dyn or i >= 2:
                    dve.wait_ge(HT_ps, i - 1)
                dve.tensor_tensor(H[:, v % 2, :], S[:, v % 2, :], B[2 + v % 2][:, P:2 * P], ALU.mult).then_inc(H_ok, 1)
                if dyn or i >= 1:
                    hidden_copy(i - 1, v - 1)
                if dyn or i + 2 < XT:
                    take_rows(i + 2, v + 2)

            take_rows(0, 0)
            take_rows(1, 1)
            groups(dve, tile_steps, XT)
            hidden_copy(XT - 1, XT - 1)
            for c in range(CH):
                dve.wait_ge(fin_ld[c], 16)
                m = dve.tensor_tensor(h[0:TP, 0:FIN_DVE, :], h[0:TP, 0:FIN_DVE, :], sums[:, c, 0:FIN_DVE, :], ALU.add)
                if c < CH - 1:
                    step(m)
            m.then_inc(fin_ok, 1)


def host_layout(a):
    f = {k: np.asarray(v) for k, v in a.items()}

    def chunks(m):
        return m.reshape(-1, P, m.shape[-1]).transpose(1, 0, 2)

    x = f["x"].reshape(IMAGES, 3, 6, 16, 6, 16).transpose(1, 3, 5, 0, 2, 4).reshape(PC * P, IMAGES, PATCHES)
    patches = np.zeros((PC * P, IMAGES, SEQ), x.dtype)
    patches[:, :, 1:] = x
    pos = np.concatenate([f["cls_tok"][0], f["L0_tok_pos_embd"][0]], 0)
    bias = np.zeros((SEQ, D), pos.dtype)
    bias[1:] = f["L0_tok_b"]
    wq, wk, wv = f["L0_attn_Wq"], f["L0_attn_Wk"], f["L0_attn_Wv"]

    def lists(gate, up, down, hidden):
        n = gate.shape[0]
        w = np.zeros((P, n, 3, 2, P), gate.dtype)
        w[:, :, 0:KC, 0, 0:hidden] = gate.reshape(n, KC, P, hidden).transpose(2, 0, 1, 3)
        w[:, :, 0:KC, 1, 0:hidden] = up.reshape(n, KC, P, hidden).transpose(2, 0, 1, 3)
        w[0:hidden, :, KC] = down.transpose(1, 0, 2).reshape(hidden, n, 2, P)
        return w.reshape(P, n * WX)

    wx = np.concatenate([lists(f["L0_ffn_w_gate"], f["L0_ffn_w_up"], f["L0_ffn_w_down"], P),
                         lists(f["L0_ffn_anchor_w_gate"], f["L0_ffn_anchor_w_up"], f["L0_ffn_anchor_w_down"], 64)], 1)
    return dict(
        pt=chunks(patches.reshape(PC * P, TOKENS)), wt=chunks(f["L0_tok_W"].T),
        posr=np.tile(pos, (3, 1)), brow=np.tile(bias, (3, 1)),
        wqkv=chunks(np.concatenate([wq, wk, wv], 1)), wo=chunks(f["L0_attn_Wo"]), wg1=chunks(f["L0_attn_Wg1"]),
        wg2=f["L0_attn_Wg2"], lnwb=chunks(np.stack([f["L0_attn_ln_w"], f["L0_attn_ln_b"]], 1)),
        gwt=chunks(f["L0_ffn_gate_weight"].T), gbias=np.tile(f["L0_ffn_gate_bias"], (P, 1)),
        sgu=chunks(np.concatenate([f["L0_ffn_shared_w_gate"], f["L0_ffn_shared_w_up"]], 1)),
        sd=f["L0_ffn_shared_w_down"], wx=wx)


def constants():
    tok = np.arange(TT)
    img, pos = tok // SEQ, tok % SEQ
    causal = ((img[:, None] == img[None]) & (pos[None] >= pos[:, None])).astype(np.float32)
    hmask = (np.arange(P)[:, None] // HD == np.arange(HEADS // KC)[None]).astype(np.float32)
    inv = (1.0 / np.float32(10000.0) ** (np.arange(0, HD, 2, dtype=np.float32) / np.float32(HD))).astype(np.float32)
    ang = pos.astype(np.float32)[:, None] * inv[None]
    cos, sin = np.cos(ang), np.sin(ang)
    cs = np.stack([np.concatenate([cos, cos], 1), np.concatenate([-sin, sin], 1)], 1)
    before = np.triu(np.ones((P, P), np.float32), 1)
    small = np.zeros((P, 2 * LISTS + 16 + 2), np.float32)
    small[:, 0:LISTS] = np.arange(LISTS)
    small[:, LISTS:2 * LISTS] = np.arange(LISTS) * LIST_ROWS
    small[:, 2 * LISTS:2 * LISTS + 16] = np.tril(np.ones((GROUPS, GROUPS)), -1).ravel()
    small[:, 2 * LISTS + 16] = np.arange(P)
    return dict(ident_c=np.eye(P, dtype=np.float32), cmask_c=causal, hmask_c=hmask, cs_c=cs.astype(np.float32),
                before_c=before, small_c=small)


def kernel(**inputs):
    import concourse.bacc as bacc
    from concourse.bass_utils import run_bass_kernel_spmd

    nc = bacc.Bacc("TRN2", target_bir_lowering=False, num_devices=1)
    arrays, args = {}, {}
    for name, a in {**host_layout(inputs), **constants()}.items():
        a = np.ascontiguousarray(a)
        arrays[f"in_{name}"] = a
        args[name] = nc.dram_tensor(f"in_{name}", a.shape, mybir.dt.from_np(a.dtype), kind="ExternalInput").ap()
    out = nc.dram_tensor("out_h", (FILL_ROW, D), F32, kind="ExternalOutput").ap()
    build(nc, **args, out=out)
    r = run_bass_kernel_spmd(nc, [arrays], core_ids=[0])
    rows = r.results[0]["out_h"].reshape(NT, TP, D)[:, :TT].reshape(NT * TT, D)
    return rows[:TOKENS].reshape(IMAGES, SEQ, D)
```

```python
from contextlib import ExitStack

import numpy as np

import concourse.bass as bass
from concourse import mybir

F32 = mybir.dt.float32
I32 = mybir.dt.int32
U32 = mybir.dt.uint32
ALU = mybir.AluOpType
ACT = mybir.ActivationFunctionType
AX = mybir.AxisListType

P = 128
D = 256
KC = D // P
IMAGES, PATCHES = 32, 36
SEQ = PATCHES + 1
TOKENS = IMAGES * SEQ
PC = 3 * 16 * 16 // P
HEADS, HD = 16, 16
TT = 3 * SEQ
TP = 112
TILES = [TT] * (IMAGES // 3) + [IMAGES % 3 * SEQ]
NT = len(TILES)
BLOCKS = [[0, 1, 2, 3], [4, 5, 6, 7], [8, 9, 10]]
BT = 4 * TT
EPS = 1e-5
EXPERTS, GROUPS, TOPK = 32, 4, 6
GE = EXPERTS // GROUPS
ANCHORS = 16
LISTS = EXPERTS + ANCHORS
CHOICES = TOPK + 1
ROUTED_SCALE, ANCHOR_ALPHA = 0.2, 0.1
HIDDEN, ANCHOR_HIDDEN = P, P // 2
UP_COLS, ANCHOR_UP_COLS = KC * 2 * HIDDEN, KC * 2 * ANCHOR_HIDDEN
WX, ANCHOR_WX = UP_COLS + D, ANCHOR_UP_COLS + D
W_COLS = EXPERTS * WX + ANCHORS * ANCHOR_WX
LIST_ROWS = TOKENS
DUMMY_ROW = LISTS * LIST_ROWS
ROW = D + LISTS + 1
ROUTED_TILES = (TOKENS * TOPK + EXPERTS * (P - 1)) // P
ANCHOR_TILES = (TOKENS + ANCHORS * (P - 1)) // P
XT = ROUTED_TILES + ANCHOR_TILES
CH = 4
FILL_ROW = NT * TP
SUM_ROWS = 11 * P
EARLY_COLS = 23276
PIECES = [(0, 4), (4, 7), (7, 9), (9, 10), (10, NT)]
assert FILL_ROW + P <= SUM_ROWS
TABLE_AFTER = 7
BIG = 3.0e38
assert CH == 4 and XT % CH == 0


def cols(t):
    return (t % 4) * TT


def build(nc, pt, wt, posr, brow, wqkv, wo, wg1, wg2, lnwb, gwt, gbias, sgu, sd, wx,
          ident_c, cmask_c, hmask_c, cs_c, before_c, small_c, out):
    with ExitStack() as ctx:
        def sb(name, shape, dt=F32):
            return ctx.enter_context(nc.sbuf_tensor(name, shape, dt))

        def sem(name):
            return ctx.enter_context(nc.semaphore(name))

        W = sb("W", [P, W_COLS])
        taken = [W_COLS - EARLY_COLS]
        late = [taken[0]]

        def early(shape):
            n = int(np.prod(shape))
            v = W[:, taken[0]:taken[0] + n]
            taken[0] += n
            assert taken[0] <= W_COLS
            if len(shape) == 2:
                return v.rearrange("p (a b) -> p a b", b=shape[1])
            if len(shape) == 3:
                return v.rearrange("p (a b c) -> p a b c", b=shape[1], c=shape[2])
            return v

        patches = early([2, PC, BT])
        w_patch = early([PC, D])
        posb = early([D])[0:TT]
        brow_sb = early([D])[0:TT]
        late.append(taken[0])
        w_qkv = early([KC, 3 * D])
        w_g2 = early([D])[0:HD]
        xnT = early([KC, BT])
        qk = early([4, 2 * D])
        rp = early([2, 2 * D])
        v_sb = early([4, D])
        qT = early([2, KC, TT])
        kT = early([2, KC, TT])
        q_heads = early([2, HEADS, TT])
        gate_th = early([4, D])
        late.append(taken[0])
        xn = early([4, D])
        w_o = early([KC, D])
        ynT = early([2, KC, TT])
        oh = early([4, CHOICES, LISTS])
        prod = early([CHOICES, LISTS])
        late.append(W_COLS)
        assert taken[0] == W_COLS

        w_g1 = sb("w_g1", [P, KC, HD])
        ln_wb = sb("ln_wb", [P, KC, 2])
        w_route = sb("w_route", [P, KC, EXPERTS])
        bias_rt = sb("bias_rt", [P, EXPERTS])
        w_sgu = sb("w_sgu", [P, KC, D])
        w_sd = sb("w_sd", [P, D])
        ident = sb("ident", [P, P])
        causal = sb("causal", [TT, TT])
        hmask = sb("hmask", [P, HEADS // KC])
        cossin = sb("cossin", [TT, 2, HD])
        before = sb("before", [P, P])
        ones = sb("ones", [P, P])
        small = sb("small", [P, 3 * LISTS + 16 + 2])
        iota_l, base0, tri4, pcol = (small[:, 0:LISTS], small[:, LISTS:2 * LISTS],
                                     small[:, 2 * LISTS:2 * LISTS + 16], small[:, 2 * LISTS + 16:2 * LISTS + 17])
        w_start = small[:, 2 * LISTS + 17:3 * LISTS + 17]
        h = sb("h", [P, NT, D])
        xrow = sb("xrow", [P, NT, ROW])
        xrow_i = xrow[:, :, :].bitcast(I32)
        x2T = sb("x2T", [P, KC, TOKENS])
        g1T = sb("g1T", [HD, 2, TT])
        e_sb = sb("e_sb", [P, 2 * HEADS * TT])
        energy = e_sb[:, :].rearrange("p (u h t) -> p u h t", u=2, h=HEADS)
        stats = sb("stats", [P, 4, 6])
        mv = sb("mv", [P, 2, 4, 2])
        nwt = sb("nwt", [P, 4, 4])
        nwt_i = nwt[:, :, :].bitcast(I32)
        sig = sb("sig", [P, 4, EXPERTS])
        sc = sb("sc", [P, 4, EXPERTS])
        top8 = sb("top8", [P, 4 * GROUPS, 8])
        gs = sb("gs", [P, 3, 4 * GROUPS])
        cmp = sb("cmp", [P, 2, 4, GROUPS, GROUPS])
        tv = sb("tv", [P, 4, 8])
        ti = sb("ti", [P, 4, 8], U32)
        ai = sb("ai", [P, 4], U32)
        idx = sb("idx", [P, 4, CHOICES])
        chosen = sb("chosen", [P, 4, LISTS])
        base = sb("base", [P, LISTS])
        rnk = sb("rnk", [P, LISTS])
        slot_f = sb("slot_f", [P, CHOICES])
        slot = sb("slot", [P, NT, CHOICES], I32)
        wsum = sb("wsum", [P, 2, 4])
        cnt_i = sb("cnt_i", [P, LISTS], I32)
        tabf = sb("tabf", [P, 6, LISTS])
        tcol = sb("tcol", [P, 8])
        table = sb("table", [1, 3, P], I32)
        fresh, dups = (v[:, :, :].rearrange("p k e -> p (k e)") for v in (sig, sc))
        padrow = sb("padrow", [P, ROW])
        padrow_i = padrow[:, :].bitcast(I32)
        at = [0]

        def later(n):
            v = e_sb[:, at[0]:at[0] + n]
            at[0] += n
            assert at[0] <= 2 * HEADS * TT
            return v

        G = later(4 * ROW).rearrange("p (u r) -> p u r", u=4)
        GT = later(2 * D).rearrange("p (u k s) -> p u k s", u=2, k=KC)
        S = later(2 * P).rearrange("p (u s) -> p u s", u=2)
        H = later(2 * P).rearrange("p (u s) -> p u s", u=2)
        HT = later(2 * P).rearrange("p (u s) -> p u s", u=2)
        UPW = sb("UPW", [P, 2, UP_COLS])
        Y = later(4 * D).rearrange("p (u s) -> p u s", u=4)
        G_i = G.bitcast(I32)
        wcol = sb("wcol", [P, XT])
        tok_of = sb("tok_of", [P, XT], I32)
        tok = sb("tok", [P, CH], I32)
        sums = W[0:TP, 0:CH * NT * D].rearrange("p (c t d) -> p c t d", c=CH, t=NT)

        B = [ctx.enter_context(nc.psum_tensor(f"B{i}", [P, 512], F32)) for i in range(8)]

        rows_d = nc.dram_tensor("rows_d", [DUMMY_ROW + P, ROW], F32).ap()
        sums_d = [nc.dram_tensor(f"sums{c}_d", [SUM_ROWS, D], F32).ap() for c in range(CH)]

        ld = {n: sem(f"ld_{n}") for n in ("patch1", "patch2", "first", "consts", "rest", "lists", "late0", "late1", "late2")}
        chunk = [sem(f"chunk{c}") for c in range(PC)]
        h_emb, xn_ok, xnT_ok = sem("h_emb"), sem("xn_ok"), sem("xnT_ok")
        emb_ps, xnT_ps, qk_ps, v_ps = sem("emb_ps"), sem("xnT_ps"), sem("qk_ps"), sem("v_ps")
        qk_ok, v_ok, g1_ps, g1_ok = sem("qk_ok"), sem("v_ok"), sem("g1_ps"), sem("g1_ok")
        gate_ps, gate_ok, rope_ok = sem("gate_ps"), sem("gate_ok"), sem("rope_ok")
        qkT_ps, qh_ok, qkT_ok = sem("qkT_ps"), sem("qh_ok"), sem("qkT_ok")
        en_ps, en_ok, av_ps, og_ok = sem("en_ps"), sem("en_ok"), sem("av_ps"), sem("og_ok")
        yn_ok, ynT_ps, ynT_ok, wo_ps, h2_ok = sem("yn_ok"), sem("ynT_ps"), sem("ynT_ok"), sem("wo_ps"), sem("h2_ok")
        x2_ok, x2T_ps, x2T_ok = sem("x2_ok"), sem("x2T_ps"), sem("x2T_ok")
        rt_ps, rt_ok, ch_ok, ch_done, rank_ps, slot_ok = (sem("rt_ps"), sem("rt_ok"), sem("ch_ok"), sem("ch_done"), sem("rank_ps"), sem("slot_ok"))
        dchain, ln_ok = sem("dchain"), sem("ln_ok")
        ini, ini_d = sem("ini"), sem("ini_d")
        scat, scat_anchor, empty = sem("scat"), sem("scat_anchor"), sem("empty")
        cols_ok, table_ps, table_ok = sem("cols_ok"), sem("table_ps"), sem("table_ok")
        sgu_ps, ssilu_ok, sh_ok, shT_ps, shT_ok, sd_ps, hs_ok = (
            sem("sgu_ps"), sem("ssilu_ok"), sem("sh_ok"), sem("shT_ps"), sem("shT_ok"), sem("sd_ps"), sem("hs_ok"))
        g_ld = [sem(f"g_ld{u}") for u in range(4)]
        T_ps, gt_ok, U_ps, silu_ok, H_ok, upw_ok, D_ps, Y_ok = (
            sem("T_ps"), sem("gt_ok"), sem("U_ps"), sem("silu_ok"), sem("H_ok"), sem("upw_ok"), sem("D_ps"), sem("Y_ok"))
        added = [sem(f"added{c}") for c in range(CH)]
        meta_ok = sem("meta_ok")
        fin_ld = [(sem(f"fin_ld{q}a"), sem(f"fin_ld{q}b")) for q in range(len(PIECES))]
        fin_ok, fin_pair, out_st = sem("fin_ok"), sem("fin_pair"), sem("out_st")
        block = ctx.enter_context(nc.Block())

        def is_anchor(i, anchor):
            return i >= ROUTED_TILES if isinstance(i, int) else anchor

        def groups(eng, body):
            def straight(lo, hi):
                for i in range(lo, hi):
                    body(i, i, i >= ROUTED_TILES)

            def loop(lo, hi, anchor):
                with eng.Fori(lo // 4, hi // 4) as j:
                    for u in range(4):
                        body(4 * j + u, u + 4, anchor)

            last_routed = (ROUTED_TILES - 2) // 4 * 4
            first_anchor = -(-(ROUTED_TILES + 2) // 4) * 4
            straight(0, 4)
            loop(4, last_routed, False)
            straight(last_routed, first_anchor)
            loop(first_anchor, XT - 4, True)
            straight(XT - 4, XT)

        def entry(engine, q, i, top):
            return nc.values_load(table[0:1, q, bass.ds(i, 1)], engines=(engine,), min_val=0, max_val=top,
                                  skip_runtime_bounds_check_because="the table is computed within these bounds")

        def load_chunk(eng, c):
            eng.dma_start(w_patch[:, c, :], wt[:, c, :]).then_inc(chunk[c], 16)
            eng.dma_start(patches[:, 0, c, :], pt[:, c, 0:BT]).then_inc(chunk[c], 16)

        EMBED_BANK = [0, 1, 2, 3]
        EMBED_BANK_LATER = [7, 6, 7, 6]

        def up_bank(t):
            return B[(6 if t < 4 else 4) + t % 2]

        @block.sync
        def _(sp):
            def load_patches(b):
                n = sum(TILES[t] for t in BLOCKS[b])
                sp.dma_start(patches[:, b % 2, :, 0:n], pt[:, :, b * BT:b * BT + n]).then_inc(ld[f"patch{b}"], 16)

            for c in range(0, PC, 2):
                load_chunk(sp, c)
            for dst, src in ((posb, posr), (brow_sb, brow)):
                sp.dma_start(dst[:, :], src).then_inc(ld["first"], 16)
            for dst, src in ((ident, ident_c), (small, small_c)):
                sp.dma_start(dst[:, :], src).then_inc(ld["consts"], 16)
            sp.dma_start(w_qkv[:, :, :], wqkv).then_inc(ld["consts"], 16)
            sp.dma_start(cossin[:, :, :], cs_c).then_inc(ld["consts"], 16)
            for dst, src in ((causal, cmask_c), (hmask, hmask_c), (before, before_c), (w_g2, wg2), (bias_rt, gbias),
                             (w_sd, sd)):
                sp.dma_start(dst[:, :], src).then_inc(ld["rest"], 16)
            for dst, src in ((w_o, wo), (w_g1, wg1), (ln_wb, lnwb), (w_route, gwt), (w_sgu, sgu)):
                sp.dma_start(dst[:, :, :], src).then_inc(ld["rest"], 16)
            load_patches(1)
            sp.wait_ge(ini, 4)
            sp.dma_start(rows_d[0:DUMMY_ROW, :].rearrange("(l r) n -> r l n", r=LIST_ROWS)[0:P, :, :],
                         padrow[:, :].unsqueeze(1).to_broadcast([P, LISTS, ROW])).then_inc(empty, 16)
            sp.dma_start(W[:, 0:late[0]], wx[:, 0:late[0]]).then_inc(ld["lists"], 16)
            for c in range(CH):
                sp.dma_start(sums_d[c].rearrange("(a p) n -> p a n", p=P),
                             padrow[:, 0:D].unsqueeze(1).to_broadcast([P, SUM_ROWS // P, D])).then_inc(ini_d, 16)
            sp.dma_start(rows_d[DUMMY_ROW:DUMMY_ROW + P, :], padrow[:, :]).then_inc(ini_d, 16)
            sp.wait_ge(emb_ps, len(BLOCKS[0]))
            load_patches(2)

            def load_late(part):
                lo, hi = late[part], late[part + 1]
                sp.dma_start(W[:, lo:hi], wx[:, lo:hi]).then_inc(ld[f"late{part}"], 16)

            sp.wait_ge(h_emb, NT)
            load_late(0)
            sp.wait_ge(og_ok, NT)
            load_late(1)
            sp.wait_ge(slot_ok, NT)
            load_late(2)
            sp.wait_ge(scat, 16 * NT * TOPK)
            sp.wait_ge(ini_d, 16 * (CH + 1))
            sp.wait_ge(table_ok, 1)

            def load_rows(i, u, anchor):
                if isinstance(i, int) and i == ROUTED_TILES:
                    sp.wait_ge(scat_anchor, 16 * NT)
                if not isinstance(i, int) or i >= 4:
                    sp.wait_ge(T_ps, i - 3)
                    sp.wait_ge(meta_ok, i - 3)
                else:
                    sp.wait_ge(en_ok, 4 * NT)
                row = entry(mybir.EngineType.SP, 1, i, DUMMY_ROW)
                sp.dma_start(G[:, u % 4, :], rows_d[bass.ds(row, P), :]).then_inc(g_ld[u % 4], 16)

            groups(sp, load_rows)
            sp.wait_ge(D_ps, XT)
            for q, (lo, hi) in enumerate(PIECES):
                for c in range(CH):
                    if q == 0:
                        sp.wait_ge(added[c], 16 * (XT // CH))
                    sp.dma_start(sums[:, c, lo:hi, :], sums_d[c][lo * TP:hi * TP, :]
                                 .rearrange("(t p) n -> p t n", p=TP)).then_inc(fin_ld[q][c // 2], 16)
            out_v = out.rearrange("(t p) n -> p t n", p=TP)
            for q, (lo, hi) in enumerate(PIECES):
                sp.wait_ge(fin_ok, q + 1)
                sp.dma_start(out_v[:, lo:hi, :], h[0:TP, lo:hi, :]).then_inc(out_st, 16)
            sp.wait_ge(out_st, 16 * len(PIECES))

        @block.gpsimd
        def _(pool):
            pool.memset(ones[:, :], 1.0).then_inc(ini, 1)
            pool.memset(padrow[:, 0:ROW - 1], 0.0)
            pool.iota(padrow_i[:, ROW - 1:ROW], pattern=[[0, 1]], base=FILL_ROW, channel_multiplier=1).then_inc(ini, 1)
            pool.memset(xrow[:, :, D + EXPERTS:D + LISTS], ANCHOR_ALPHA)
            pool.iota(xrow_i[:, :, ROW - 1], pattern=[[TP, NT]], base=0, channel_multiplier=1).then_inc(ini, 1)
            pool.memset(h[:, :, :], 0.0).then_inc(ini, 1)
            pool.wait_ge(ini, 4)
            pool.wait_ge(ld["rest"], 16 * 11)

            def split_heads(t):
                n = TILES[t]
                pool.wait_ge(qkT_ok, t + 1)
                if t >= 2:
                    pool.wait_ge(en_ps, 4 * (t - 1))
                for k in range(KC):
                    pool.tensor_tensor(q_heads[:, t % 2, 8 * k:8 * k + 8, 0:n],
                                       qT[:, t % 2, k, 0:n].unsqueeze(1).to_broadcast([P, 8, n]),
                                       hmask[:, :].unsqueeze(2).to_broadcast([P, 8, n]), ALU.mult).then_inc(qh_ok, 1)

            def scatter(t, choices, done):
                n = TILES[t]
                for j in choices:
                    pool.indirect_dma_start(rows_d, bass.IndirectOffsetOnAxis(ap=slot[0:n, t, j:j + 1], axis=0),
                                            xrow[0:n, t, :], None).then_inc(done, 16)

            for b, tiles in enumerate(BLOCKS):
                for t in tiles:
                    split_heads(t)
                if b == 1:
                    pool.wait_ge(empty, 16)
                if b:
                    for t in BLOCKS[b - 1]:
                        pool.wait_ge(slot_ok, t + 1)
                        scatter(t, range(TOPK), scat)
                        scatter(t, [TOPK], scat_anchor)
            for t in BLOCKS[-1]:
                pool.wait_ge(slot_ok, t + 1)
                scatter(t, range(TOPK), scat)
            for t in BLOCKS[-1]:
                scatter(t, [TOPK], scat_anchor)

            def add_rows(i, u, anchor):
                c = u % CH
                pool.wait_ge(Y_ok, i + 1)
                pool.nop(nofuse=True)
                pool.indirect_dma_start(sums_d[c], bass.IndirectOffsetOnAxis(ap=tok[:, c:c + 1], axis=0),
                                        Y[:, c, :], None, compute_op=ALU.add).then_inc(added[c], 16)

            groups(pool, add_rows)
            for q, (lo, hi) in enumerate(PIECES):
                pool.wait_ge(fin_ld[q][1], 16 * 2)
                pool.tensor_tensor(sums[:, 2, lo:hi, :], sums[:, 2, lo:hi, :], sums[:, 3, lo:hi, :],
                                   ALU.add).then_inc(fin_pair, 1)

        @block.tensor
        def _(pe):
            def out_project(t):
                n = TILES[t]
                pe.wait_ge(ynT_ok, t + 1)
                if t >= 2:
                    pe.wait_ge(h2_ok, t - 1)
                for k in range(KC):
                    m = pe.matmul(B[4 + t % 2][0:n, 0:D], ynT[:, t % 2, k, 0:n], w_o[:, k, :],
                                  start=k == 0, stop=k == KC - 1)
                m.then_inc(wo_ps, 1)

            def route(t):
                n, r = TILES[t], t * TT
                pe.wait_ge(x2T_ok, t + 1)
                if t >= 2:
                    pe.wait_ge(rt_ok, t - 1)
                for k in range(KC):
                    m = pe.matmul(B[t % 2][0:n, 0:EXPERTS], x2T[:, k, r:r + n], w_route[:, k, :],
                                  start=k == 0, stop=k == KC - 1)
                m.then_inc(rt_ps, 1)

            def rank(t):
                n, at = TILES[t], t % 4 * P
                pe.wait_ge(ch_ok, t + 1)
                pe.matmul(B[7][0:n, at:at + LISTS], before[0:n, 0:n], chosen[0:n, t % 4, :], start=True, stop=True)
                pe.matmul(B[7][:, at + LISTS:at + 2 * LISTS], ones[0:n, :], chosen[0:n, t % 4, :],
                          start=True, stop=True).then_inc(rank_ps, 1)

            def embed(t, bank):
                n, b = TILES[t], t // 4
                pe.wait_ge(ld[f"patch{b}"], 16)
                for c in range(PC):
                    m = pe.matmul(B[bank][0:n, 0:D], patches[:, b % 2, c, cols(t):cols(t) + n], w_patch[:, c, :],
                                  start=c == 0, stop=c == PC - 1)
                m.then_inc(emb_ps, 1)

            def transpose2(bank, src, n, done):
                for k in range(KC):
                    m = pe.transpose(bank[:, k * TT:k * TT + n], src[0:n, k * P:(k + 1) * P], ident[0:n, 0:n])
                m.then_inc(done, 1)

            def project(t):
                n = TILES[t]
                for ps, lo, hi, done in ((B[4 + t % 2], 0, 2 * D, qk_ps), (B[6 + t % 2], 2 * D, 3 * D, v_ps)):
                    for k in range(KC):
                        m = pe.matmul(ps[0:n, 0:hi - lo], xnT[:, k, cols(t):cols(t) + n], w_qkv[:, k, lo:hi],
                                      start=k == 0, stop=k == KC - 1)
                    m.then_inc(done, 1)
                if t >= 2:
                    pe.wait_ge(gate_ok, t - 1)
                for k in range(KC):
                    m = pe.matmul(B[t % 2][0:HD, D:D + n], w_g1[:, k, :], xnT[:, k, cols(t):cols(t) + n],
                                  start=k == 0, stop=k == KC - 1)
                m.then_inc(g1_ps, 1)

            def gate(t):
                n = TILES[t]
                pe.wait_ge(g1_ok, t + 1)
                if t >= 2:
                    pe.wait_ge(gate_ok, t - 1)
                pe.matmul(B[t % 2][0:n, 0:D], g1T[:, t % 2, 0:n], w_g2[:, :], start=True, stop=True).then_inc(gate_ps, 1)

            def qk_transpose(t):
                n = TILES[t]
                pe.wait_ge(rope_ok, t + 1)
                if t >= 2:
                    pe.wait_ge(qkT_ok, t - 1)
                for k in range(2 * KC):
                    m = pe.transpose(B[2 + t % 2][:, k * TT:k * TT + n], qk[0:n, t % 4, k * P:(k + 1) * P],
                                     ident[0:n, 0:n])
                m.then_inc(qkT_ps, 1)

            def energies(t):
                n = TILES[t]
                for g in range(4):
                    i = 4 * t + g
                    if g % 2 == 0:
                        pe.wait_ge(qh_ok, 2 * t + g // 2 + 1)
                    if i >= 3:
                        pe.wait_ge(en_ok, i - 2)
                    pe.matmul(B[4 + i % 3][0:n, 0:4 * n], kT[:, t % 2, g // 2, 0:n],
                              q_heads[:, t % 2, 4 * g:4 * g + 4, 0:n],
                              start=True, stop=True).then_inc(en_ps, 1)

            def attend(t):
                n = TILES[t]
                pe.wait_ge(en_ok, 4 * t + 4)
                if t >= 2:
                    pe.wait_ge(og_ok, t - 1)
                for hd in range(HEADS):
                    m = pe.matmul(B[t % 2][0:n, hd * HD:(hd + 1) * HD], energy[0:n, t % 2, hd, 0:n],
                                  v_sb[0:n, t % 4, hd * HD:(hd + 1) * HD], start=True, stop=True)
                m.then_inc(av_ps, 1)

            def s_up(t):
                n, r = TILES[t], t * TT
                if t >= 2:
                    pe.wait_ge(sh_ok, t - 1)
                for k in range(KC):
                    m = pe.matmul(up_bank(t)[0:n, 0:D], x2T[:, k, r:r + n], w_sgu[:, k, :],
                                  start=k == 0, stop=k == KC - 1)
                m.then_inc(sgu_ps, 1)

            def s_transpose(t):
                n = TILES[t]
                pe.wait_ge(sh_ok, t + 1)
                if t >= 2:
                    pe.wait_ge(shT_ok, t - 1)
                pe.transpose(B[2 + t % 2][:, 0:n], H[0:n, t % 2, :], ident[0:n, 0:n]).then_inc(shT_ps, 1)

            def s_down(t):
                n = TILES[t]
                pe.wait_ge(shT_ok, t + 1)
                if t >= 2:
                    pe.wait_ge(hs_ok, t - 1)
                pe.matmul(B[t % 2][0:n, 0:D], HT[:, t % 2, 0:n], w_sd[:, :],
                          start=True, stop=True).then_inc(sd_ps, 1)

            for tiles, c in [(BLOCKS[0][:3], c) for c in range(PC)] + [(BLOCKS[0][3:], c) for c in range(PC)]:
                pe.wait_ge(chunk[c], 32)
                for t in tiles:
                    m = pe.matmul(B[EMBED_BANK[t]][0:TILES[t], 0:D], patches[:, 0, c, cols(t):cols(t) + TILES[t]],
                                  w_patch[:, c, :], start=c == 0, stop=c == PC - 1)
                    if c == PC - 1:
                        m.then_inc(emb_ps, 1)
            pe.wait_ge(ld["consts"], 16 * 4)
            pe.wait_ge(ini, 4)
            for b, tiles in enumerate(BLOCKS):
                t0, t1 = tiles[0], tiles[-1] + 1
                for t in tiles:
                    pe.wait_ge(xn_ok, t + 1)
                    if t >= 2:
                        pe.wait_ge(xnT_ok, t - 1)
                    transpose2(B[2 + t % 2], xn[:, t % 4, :], TILES[t], xnT_ps)
                if b == 0:
                    pe.wait_ge(ld["rest"], 16 * 11)
                else:
                    pe.wait_ge(rt_ok, t0)
                for t in tiles:
                    pe.wait_ge(xnT_ok, t + 1)
                    if t >= 2:
                        pe.wait_ge(qk_ok, t - 1)
                        pe.wait_ge(v_ok, t - 1)
                        pe.wait_ge(g1_ok, t - 1)
                    project(t)
                    if t > t0:
                        gate(t - 1)
                    if t == t0 + 2:
                        qk_transpose(t0)
                gate(t1 - 1)
                qk_transpose(t0 + 1)
                if b:
                    pe.wait_ge(v_ok, t1)
                    for t in BLOCKS[b - 1]:
                        rank(t)
                pe.wait_ge(qk_ok, t1)
                pe.wait_ge(v_ok, t1)
                for t in tiles:
                    if t > t0 and t + 1 < t1:
                        qk_transpose(t + 1)
                    energies(t)
                    if t == t0:
                        pe.wait_ge(gate_ok, t1)
                    if t > t0:
                        attend(t - 1)
                following = BLOCKS[b + 1] if b + 1 < len(BLOCKS) else []
                if following:
                    if b:
                        pe.wait_ge(slot_ok, t0)
                    embed(t1, EMBED_BANK_LATER[0])
                attend(t1 - 1)
                if following:
                    embed(t1 + 1, EMBED_BANK_LATER[1])
                else:
                    pe.wait_ge(slot_ok, t0)
                    s_up(0)
                    s_up(1)
                for t in tiles:
                    pe.wait_ge(yn_ok, t + 1)
                    if t >= 2:
                        pe.wait_ge(ynT_ok, t - 1)
                    transpose2(B[2 + t % 2], xn[:, t % 4, :], TILES[t], ynT_ps)
                    if t > t0:
                        out_project(t - 1)
                out_project(t1 - 1)
                for t in following[2:]:
                    pe.wait_ge(h_emb, t - 1)
                    embed(t, EMBED_BANK_LATER[t % 4])
                if not following:
                    pe.wait_ge(ynT_ok, t1)
                    pe.wait_ge(og_ok, t1)
                    s_transpose(0)
                    s_transpose(1)
                    s_down(0)
                    s_down(1)
                    s_up(2)
                    s_up(3)
                    pe.wait_ge(shT_ok, 2)
                    pe.wait_ge(hs_ok, 2)
                for t in tiles:
                    pe.wait_ge(x2_ok, t + 1)
                    if t >= 2:
                        pe.wait_ge(x2T_ok, t - 1)
                    transpose2(B[2 + t % 2], xrow[:, t, :], TILES[t], x2T_ps)
                    if t > t0:
                        route(t - 1)
                route(t1 - 1)

            def table_rows():
                pe.wait_ge(cols_ok, 1)
                for q in range(3):
                    pe.matmul(B[6][0:1, q * P:(q + 1) * P], tcol[:, q:q + 1], ident[:, :], start=True, stop=True)
                pe.matmul(B[6][:, 3 * P:4 * P], ones[:, :], dups[:, :], start=True, stop=True).then_inc(table_ps, 1)

            pe.wait_ge(h2_ok, NT)
            pe.wait_ge(rt_ok, NT)
            s_transpose(2)
            s_transpose(3)
            s_up(4)
            s_up(5)
            s_down(2)
            s_down(3)
            for t in BLOCKS[-1]:
                rank(t)
            for t in range(6, NT):
                s_transpose(t - 2)
                s_up(t)
                s_down(t - 2)
                if t == TABLE_AFTER:
                    table_rows()
            s_transpose(NT - 2)
            s_transpose(NT - 1)
            s_down(NT - 2)
            s_down(NT - 1)
            pe.wait_ge(ld["lists"], 16)
            for part in range(3):
                pe.wait_ge(ld[f"late{part}"], 16)
            pe.wait_ge(table_ok, 1)
            pe.wait_ge(hs_ok, NT)
            pe.wait_ge(shT_ok, NT)

            def turn_rows(i, u):
                pe.wait_ge(g_ld[u % 4], (i - u % 4) * 4 + 16)
                for k in range(KC):
                    m = pe.transpose(B[u % 2][:, k * P:(k + 1) * P], G[:, u % 4, k * P:(k + 1) * P], ident[:, :])
                m.then_inc(T_ps, 1)

            def up(i, u, anchor):
                pe.wait_ge(gt_ok, i + 1)
                pe.wait_ge(upw_ok, i + 1)
                parts = 1 if anchor else 2
                for m in range(parts):
                    for k in range(KC):
                        at = (k * parts + m) * P
                        mm = pe.matmul(B[2 + u % 2][:, m * P:(m + 1) * P], UPW[:, u % 2, at:at + P], GT[:, u % 2, k, :],
                                       start=k == 0, stop=k == KC - 1)
                mm.then_inc(U_ps, 1)

            def down(i, u, anchor):
                size, at = (ANCHOR_WX, ANCHOR_UP_COLS) if anchor else (WX, UP_COLS)
                e = entry(mybir.EngineType.PE, 0, i, W_COLS - size)
                pe.wait_ge(H_ok, i + 1)
                pe.matmul(B[6 + u % 2][:, 0:D], H[:, u % 2, :], W[:, bass.ds(e, size)][:, at:at + D],
                          start=True, stop=True).then_inc(D_ps, 1)

            def list_tile(i, u, anchor):
                up(i, u, anchor)
                if not isinstance(i, int) or i + 2 < XT:
                    turn_rows(i + 2, u + 2)
                if not isinstance(i, int) or i >= 1:
                    down(i - 1, u - 1, is_anchor(i - 1, anchor))

            turn_rows(0, 0)
            turn_rows(1, 1)
            groups(pe, list_tile)
            down(XT - 1, XT - 1, True)

        @block.scalar
        def _(act):
            for c in range(1, PC, 2):
                load_chunk(act, c)

            def gate_tanh(t):
                n = TILES[t]
                act.wait_ge(gate_ps, t + 1)
                act.activation(gate_th[0:n, t % 4, :], B[t % 2][0:n, 0:D], ACT.Tanh, scale=0.5).then_inc(gate_ok, 1)

            def copy2(dst, bank, n, s, v, done):
                act.wait_ge(s, v)
                act.copy(dst, bank[:, 0:KC * TT].rearrange("p (k t) -> p k t", k=KC)[:, :, 0:n]).then_inc(done, 1)

            def normal(dst, src, t, done):
                n = TILES[t]
                act.activation(dst, src, ACT.Identity, scale=nwt[0:n, 1, t % 4:t % 4 + 1],
                               bias=nwt[0:n, 3, t % 4:t % 4 + 1]).then_inc(done, 1)

            def s_silu(t):
                n = TILES[t]
                act.wait_ge(sgu_ps, t + 1)
                if t >= 2:
                    act.wait_ge(sh_ok, t - 1)
                act.activation(S[0:n, t % 2, :], up_bank(t)[0:n, 0:P], ACT.Silu).then_inc(ssilu_ok, 1)

            def s_copy(t):
                n = TILES[t]
                act.wait_ge(shT_ps, t + 1)
                if t >= 2:
                    act.wait_ge(sd_ps, t - 1)
                act.copy(HT[:, t % 2, 0:n], B[2 + t % 2][:, 0:n]).then_inc(shT_ok, 1)

            def qk_copy(t):
                n = TILES[t]
                act.wait_ge(qkT_ps, t + 1)
                if t >= 2:
                    act.wait_ge(en_ps, 4 * (t - 1))
                act.copy(qT[:, t % 2, :, 0:n], B[2 + t % 2][:, 0:KC * TT]
                         .rearrange("p (k t) -> p k t", k=KC)[:, :, 0:n])
                act.copy(kT[:, t % 2, :, 0:n], B[2 + t % 2][:, KC * TT:2 * KC * TT]
                         .rearrange("p (k t) -> p k t", k=KC)[:, :, 0:n]).then_inc(qkT_ok, 1)

            for b, tiles in enumerate(BLOCKS):
                t0, t1 = tiles[0], tiles[-1] + 1

                def x_copy(t):
                    copy2(xnT[:, :, cols(t):cols(t) + TILES[t]], B[2 + t % 2], TILES[t], xnT_ps, t + 1, xnT_ok)

                act.wait_ge(ln_ok, 3 * b + 1)
                if b:
                    act.wait_ge(ynT_ps, t0)
                for t in tiles:
                    normal(xn[0:TILES[t], t % 4, :], h[0:TILES[t], t, :], t, xn_ok)
                    if t > t0:
                        x_copy(t - 1)
                x_copy(t1 - 1)
                for t in tiles:
                    n = TILES[t]
                    act.wait_ge(qk_ps, t + 1)
                    act.activation(qk[0:n, t % 4, :], B[4 + t % 2][0:n, :], ACT.Silu).then_inc(qk_ok, 1)
                    act.wait_ge(v_ps, t + 1)
                    act.copy(v_sb[0:n, t % 4, :], B[6 + t % 2][0:n, 0:D]).then_inc(v_ok, 1)
                    act.wait_ge(g1_ps, t + 1)
                    if t >= 2:
                        act.wait_ge(gate_ps, t - 1)
                    act.copy(g1T[:, t % 2, 0:n], B[t % 2][0:HD, D:D + n]).then_inc(g1_ok, 1)
                    if t > t0:
                        gate_tanh(t - 1)
                    if t == t0 + 2:
                        qk_copy(t0)
                gate_tanh(t1 - 1)
                for t in tiles[1:]:
                    qk_copy(t)

                def yn_copy(t):
                    n = TILES[t]
                    act.wait_ge(ynT_ps, t + 1)
                    if t >= 2:
                        act.wait_ge(wo_ps, t - 1)
                    for k in range(KC):
                        m = act.activation(ynT[:, t % 2, k, 0:n], B[2 + t % 2][:, k * TT:k * TT + n], ACT.Identity,
                                           scale=ln_wb[:, k, 0:1], bias=ln_wb[:, k, 1:2])
                    m.then_inc(ynT_ok, 1)

                if t1 == NT:
                    s_silu(0)
                    s_silu(1)
                act.wait_ge(ln_ok, 3 * b + 2)
                for t in tiles:
                    normal(xn[0:TILES[t], t % 4, :], xn[0:TILES[t], t % 4, :], t, yn_ok)
                    if t > t0:
                        yn_copy(t - 1)
                yn_copy(t1 - 1)

                def x2_copy(t):
                    n, r = TILES[t], t * TT
                    copy2(x2T[:, :, r:r + n], B[2 + t % 2], n, x2T_ps, t + 1, x2T_ok)

                if t1 == NT:
                    s_copy(0)
                    s_copy(1)
                    s_silu(2)
                    s_silu(3)
                act.wait_ge(ln_ok, 3 * b + 3)
                for t in tiles:
                    normal(xrow[0:TILES[t], t, 0:D], h[0:TILES[t], t, :], t, x2_ok)
                    if t > t0:
                        x2_copy(t - 1)
                x2_copy(t1 - 1)
                for t in tiles:
                    n = TILES[t]
                    act.wait_ge(rt_ps, t + 1)
                    if b:
                        act.wait_ge(ch_done, b)
                    act.activation(sig[0:n, t % 4, :], B[t % 2][0:n, 0:EXPERTS], ACT.Sigmoid).then_inc(rt_ok, 1)
            for t in (2, 3):
                s_copy(t)
            for t in (4, 5):
                s_silu(t)
            for t in range(6, NT):
                s_copy(t - 2)
                s_silu(t)
            s_copy(NT - 2)
            s_copy(NT - 1)

            def list_weights(i, anchor):
                size = ANCHOR_WX if anchor else WX
                return W[:, bass.ds(entry(mybir.EngineType.Activation, 0, i, W_COLS - size), size)]

            def copy_up(weights, u, anchor):
                n = ANCHOR_UP_COLS if anchor else UP_COLS
                act.copy(UPW[:, u % 2, 0:n], weights[:, 0:n]).then_inc(upw_ok, 1)

            def hidden_silu(i, u, anchor):
                n = ANCHOR_HIDDEN if anchor else HIDDEN
                ahead = not isinstance(i, int) or i + 2 < XT
                if ahead:
                    weights = list_weights(i + 2, is_anchor(i + 2, anchor))
                act.wait_ge(U_ps, i + 1)
                act.activation(S[0:n, u % 2, :], B[2 + u % 2][0:n, 0:P], ACT.Silu).then_inc(silu_ok, 1)
                if ahead:
                    copy_up(weights, u + 2, is_anchor(i + 2, anchor))
                if not isinstance(i, int) or i >= 1:
                    weigh(i - 1, u - 1)

            def weigh(i, u):
                act.wait_ge(D_ps, i + 1)
                act.wait_ge(meta_ok, i + 1)
                if not isinstance(i, int) or i >= CH:
                    act.wait_ge(added[u % 4], (i - u % 4) * (16 // CH))
                act.copy(tok[:, u % 4:u % 4 + 1], tok_of[:, bass.ds(i, 1)])
                act.activation(Y[:, u % 4, :], B[6 + u % 2][:, 0:D], ACT.Copy, scale=wcol[:, bass.ds(i, 1)]).then_inc(Y_ok, 1)

            act.wait_ge(ld["lists"], 16)
            for part in range(3):
                act.wait_ge(ld[f"late{part}"], 16)
            act.wait_ge(table_ok, 1)
            copy_up(list_weights(0, False), 0, False)
            copy_up(list_weights(1, False), 1, False)
            groups(act, hidden_silu)
            weigh(XT - 1, XT - 1)

        @block.vector
        def _(dve):
            count, norms = [0], [0]

            def step(ins):
                count[0] += 1
                ins.then_inc(dchain, 1)
                dve.wait_ge(dchain, count[0])

            def stat(src, t, w=0):
                n = TILES[t]
                step(dve.bn_stats(stats[0:n, t % 4, :], src))
                step(dve.bn_aggr(mv[0:n, w, t % 4, :], stats[0:n, t % 4, :]))

            def deviations(k, eps, w=0):
                v, y, a = nwt[:, 0, 0:k], nwt[:, 1, 0:k], nwt[:, 2, 0:k]
                vi, yi = nwt_i[:, 0, 0:k], nwt_i[:, 1, 0:k]
                step(dve.tensor_scalar(v, mv[:, w, 0:k, 1], eps, None, ALU.add))
                step(dve.tensor_scalar(yi, vi, -0.5, float(0x5F3759DF), ALU.mult, ALU.add))
                for _ in range(3):
                    step(dve.scalar_tensor_tensor(a, y, -0.5, y, ALU.mult, ALU.mult))
                    step(dve.tensor_tensor(a, a, v, ALU.mult))
                    step(dve.scalar_tensor_tensor(y, a, 1.5, y, ALU.add, ALU.mult))
                norms[0] += 1
                dve.scalar_tensor_tensor(nwt[:, 3, 0:k], mv[:, w, 0:k, 0], -1.0, y, ALU.mult, ALU.mult).then_inc(ln_ok, 1)
                dve.wait_ge(ln_ok, norms[0])

            def choose(b):
                t0, k, n = BLOCKS[b][0], len(BLOCKS[b]), TT
                t1 = t0 + k
                s, sct = sig[0:n, 0:k, :], sc[0:n, 0:k, :]
                g0, g1, g2 = (gs[0:n, q, 0:GROUPS * k] for q in range(3))
                by_group = sct.rearrange("p k (g e) -> p (k g) e", g=GROUPS)
                pair = [n, k, GROUPS, GROUPS]
                g0_t = g0.rearrange("p (k g) -> p k g", k=k)
                ahead, tie = cmp[0:n, 0, 0:k], cmp[0:n, 1, 0:k]

                dve.wait_ge(rt_ok, t1)
                if t0:
                    dve.wait_ge(rank_ps, t0)
                step(dve.tensor_tensor(sct, s, bias_rt[0:n, :].unsqueeze(1).to_broadcast([n, k, EXPERTS]), ALU.add))
                for g in range(GROUPS * k):
                    m = dve.max(top8[0:n, g, :], by_group[:, g, :])
                step(m)
                step(dve.tensor_tensor(g0, top8[0:n, 0:GROUPS * k, 0], top8[0:n, 0:GROUPS * k, 1], ALU.add))
                others, own = g0_t.unsqueeze(2).to_broadcast(pair), g0_t.unsqueeze(3).to_broadcast(pair)
                dve.tensor_tensor(ahead, others, own, ALU.is_gt)
                step(dve.tensor_tensor(tie, others, own, ALU.is_equal))
                step(dve.tensor_tensor(tie, tie, tri4[0:n, :].rearrange("p (a b) -> p a b", a=GROUPS)
                                       .unsqueeze(1).to_broadcast(pair), ALU.mult))
                step(dve.tensor_tensor(ahead, ahead, tie, ALU.add))
                step(dve.reduce_sum(g1.rearrange("p (k g) -> p k g", k=k), ahead, axis=AX.X))
                step(dve.tensor_scalar(g2, g1, 2.0, -BIG, ALU.is_ge, ALU.mult))
                step(dve.tensor_tensor(by_group, by_group, g2.unsqueeze(2).to_broadcast([n, GROUPS * k, GE]), ALU.add))
                for u in range(k):
                    m = dve.max(tv[0:n, u, :], sc[0:n, u, :])
                step(m)
                for u in range(k):
                    m = dve.max_index(ti[0:n, u, :], tv[0:n, u, :], sc[0:n, u, :])
                step(m)
                dve.tensor_copy(idx[0:n, 0:k, 0:TOPK], ti[0:n, 0:k, 0:TOPK])
                step(dve.tensor_scalar(ai[0:n, 0:k], ti[0:n, 0:k, 0], 1, None, ALU.logical_shift_right))
                step(dve.tensor_scalar(idx[0:n, 0:k, TOPK], ai[0:n, 0:k], float(EXPERTS), None, ALU.add))
                for u in range(k):
                    m = dve.tensor_tensor(oh[0:n, u], idx[0:n, u, :].unsqueeze(2).to_broadcast([n, CHOICES, LISTS]),
                                          iota_l[0:n, :].unsqueeze(1).to_broadcast([n, CHOICES, LISTS]), ALU.is_equal)
                step(m)
                for u in range(k):
                    dve.reduce_sum(chosen[0:n, u, :], oh[0:n, u].rearrange("p j e -> p e j"), axis=AX.X).then_inc(ch_ok, 1)
                dve.wait_ge(ch_ok, t1)
                w = xrow[0:n, t0:t1, D:D + EXPERTS]
                step(dve.tensor_tensor(w, chosen[0:n, 0:k, 0:EXPERTS], s, ALU.mult))
                step(dve.reduce_sum(wsum[0:n, 0, 0:k], w, axis=AX.X))
                step(dve.tensor_scalar(wsum[0:n, 0, 0:k], wsum[0:n, 0, 0:k], 1e-20, None, ALU.add))
                step(dve.reciprocal(wsum[0:n, 1, 0:k], wsum[0:n, 0, 0:k]))
                step(dve.tensor_scalar(wsum[0:n, 1, 0:k], wsum[0:n, 1, 0:k], ROUTED_SCALE, None, ALU.mult))
                dve.tensor_tensor(w, w, wsum[0:n, 1, 0:k].unsqueeze(2).to_broadcast([n, k, EXPERTS]),
                                  ALU.mult).then_inc(ch_done, 1)
                dve.wait_ge(ch_done, b + 1)

            def place(t, t1):
                n, at = TILES[t], t % 4 * P
                dve.wait_ge(rank_ps, t1)
                step(dve.tensor_tensor(rnk[0:n, :], B[7][0:n, at:at + LISTS], base[0:n, :], ALU.add))
                dve.tensor_tensor(base[:, :], base[:, :], B[7][:, at + LISTS:at + 2 * LISTS], ALU.add)
                step(dve.tensor_tensor(prod[0:n], oh[0:n, t % 4], rnk[0:n, :].unsqueeze(1).to_broadcast([n, CHOICES, LISTS]),
                                       ALU.mult))
                step(dve.reduce_sum(slot_f[0:n, :], prod[0:n], axis=AX.X))
                dve.tensor_copy(slot[0:n, t, :], slot_f[0:n, :]).then_inc(slot_ok, 1)
                dve.wait_ge(slot_ok, t + 1)

            def embedded(t, bank):
                n = TILES[t]
                dve.wait_ge(emb_ps, t + 1)
                dve.tensor_tensor(h[0:n, t, :], B[bank][0:n, 0:D], posb[0:n, :], ALU.add).then_inc(h_emb, 1)
                dve.wait_ge(h_emb, t + 1)

            def rope(t):
                n = TILES[t]
                dve.wait_ge(qk_ok, t + 1)
                q = qk[0:n, t % 4, :].rearrange("p (h d) -> p h d", d=HD)
                a = rp[0:n, 0, :].rearrange("p (h d) -> p h d", d=HD)
                r_ = rp[0:n, 1, :].rearrange("p (h d) -> p h d", d=HD)
                half = HD // 2

                def tab(i, lo, hi):
                    return cossin[0:n, i, lo:hi].unsqueeze(1).to_broadcast([n, 2 * HEADS, hi - lo])

                dve.tensor_tensor(a, q, tab(0, 0, HD), ALU.mult)
                dve.tensor_tensor(r_[:, :, 0:half], q[:, :, half:HD], tab(1, 0, half), ALU.mult)
                step(dve.tensor_tensor(r_[:, :, half:HD], q[:, :, 0:half], tab(1, half, HD), ALU.mult))
                dve.tensor_tensor(q, a, r_, ALU.add).then_inc(rope_ok, 1)
                dve.wait_ge(rope_ok, t + 1)

            def mask_energy(t):
                n = TILES[t]
                if t >= 2:
                    dve.wait_ge(av_ps, t - 1)
                for g in range(4):
                    i = 4 * t + g
                    dve.wait_ge(en_ps, i + 1)
                    dve.tensor_tensor(energy[0:n, t % 2, 4 * g:4 * g + 4, 0:n],
                                      B[4 + i % 3][0:n, 0:4 * n].rearrange("p (h t) -> p h t", h=4),
                                      causal[0:n, 0:n].unsqueeze(1).to_broadcast([n, 4, n]),
                                      ALU.mult).then_inc(en_ok, 1)

            def apply_gate(t):
                n = TILES[t]
                dve.wait_ge(av_ps, t + 1)
                dve.wait_ge(gate_ok, t + 1)
                dve.scalar_tensor_tensor(xn[0:n, t % 4, :], gate_th[0:n, t % 4, :], 1.0,
                                         B[t % 2][0:n, 0:D], ALU.add, ALU.mult).then_inc(og_ok, 1)
                dve.wait_ge(og_ok, t + 1)
                stat(xn[0:n, t % 4, :], t)

            def s_mult(t):
                n = TILES[t]
                dve.wait_ge(ssilu_ok, t + 1)
                if t >= 2:
                    dve.wait_ge(shT_ps, t - 1)
                dve.tensor_tensor(H[0:n, t % 2, :], S[0:n, t % 2, :], up_bank(t)[0:n, P:2 * P],
                                  ALU.mult).then_inc(sh_ok, 1)

            def s_add(t):
                n = TILES[t]
                dve.wait_ge(sd_ps, t + 1)
                dve.tensor_tensor(h[0:n, t, :], B[t % 2][0:n, 0:D], h[0:n, t, :], ALU.add).then_inc(hs_ok, 1)

            step(dve.memset(mv[:, :, :, :], 1.0))
            dve.wait_ge(ld["first"], 16 * 2)
            dve.wait_ge(ini, 4)
            step(dve.tensor_tensor(posb[:, :], posb[:, :], brow_sb[:, :], ALU.add))
            for t in BLOCKS[0]:
                embedded(t, EMBED_BANK[t % 4])
                stat(h[0:TILES[t], t, :], t)
            deviations(len(BLOCKS[0]), EPS)
            dve.wait_ge(ld["consts"], 16 * 4)
            step(dve.tensor_copy(base[:, :], base0))
            dve.wait_ge(ld["rest"], 16 * 11)
            for b, tiles in enumerate(BLOCKS):
                t0, t1 = tiles[0], tiles[-1] + 1
                if b:
                    choose(b - 1)
                for t in tiles:
                    rope(t)
                before_this = list(BLOCKS[b - 1]) if b else []
                for t in tiles:
                    mask_energy(t)
                    if before_this:
                        place(before_this.pop(0), t0)
                    if t > t0:
                        apply_gate(t - 1)
                for t in before_this:
                    place(t, t0)
                apply_gate(t1 - 1)
                dve.wait_ge(xn_ok, t1)
                deviations(len(tiles), 4 * EPS)
                following = BLOCKS[b + 1] if b + 1 < len(BLOCKS) else []
                for t in following[:2]:
                    embedded(t, EMBED_BANK_LATER[t % 4])
                    stat(h[0:TILES[t], t, :], t, 1)
                if not following:
                    s_mult(0)
                    s_mult(1)
                for t in tiles:
                    n = TILES[t]
                    dve.wait_ge(wo_ps, t + 1)
                    dve.tensor_tensor(h[0:n, t, :], B[4 + t % 2][0:n, 0:D], h[0:n, t, :], ALU.add).then_inc(h2_ok, 1)
                    dve.wait_ge(h2_ok, t + 1)
                    stat(h[0:n, t, :], t)
                dve.wait_ge(yn_ok, t1)
                deviations(len(tiles), EPS)
                for t in following[2:]:
                    embedded(t, EMBED_BANK_LATER[t % 4])
                    stat(h[0:TILES[t], t, :], t, 1)
                if not following:
                    s_add(0)
                    s_add(1)
                    s_mult(2)
                    s_mult(3)
                if following:
                    dve.wait_ge(x2_ok, t1)
                    deviations(len(following), EPS, 1)

            def shared(t):
                s_mult(t)
                s_add(t - 2)

            choose(len(BLOCKS) - 1)
            for t in BLOCKS[-1]:
                place(t, NT)
                if t < BLOCKS[-1][-1]:
                    shared(t - BLOCKS[-1][0] + 4)
            counts, tiles_of, ends, starts, mine, t5 = (tabf[:, q, :] for q in range(6))
            list_c, row_c, weight_c, start_c, over_c, base_c, used_c, dup_c = (tcol[:, q:q + 1] for q in range(8))
            step(dve.tensor_tensor(counts, base[:, :], base0, ALU.subtract))
            step(dve.tensor_scalar(cnt_i[:, :], counts, float(P - 1), None, ALU.add))
            step(dve.tensor_scalar(cnt_i[:, :], cnt_i[:, :], 7, None, ALU.logical_shift_right))
            step(dve.tensor_copy(tiles_of, cnt_i[:, :]))
            dve.tensor_tensor_scan(ends[:, 0:EXPERTS], ones[:, 0:EXPERTS], tiles_of[:, 0:EXPERTS], 0.0, ALU.mult, ALU.add)
            step(dve.tensor_tensor_scan(ends[:, EXPERTS:LISTS], ones[:, 0:ANCHORS], tiles_of[:, EXPERTS:LISTS],
                                        float(ROUTED_TILES), ALU.mult, ALU.add))
            step(dve.tensor_tensor(starts, ends, tiles_of, ALU.subtract))
            shared(6)
            dve.tensor_scalar(mine, starts, pcol, None, ALU.is_le)
            step(dve.tensor_scalar(t5, ends, pcol, None, ALU.is_gt))
            step(dve.tensor_tensor(mine, mine, t5, ALU.mult))
            step(dve.tensor_scalar(counts, counts, -float(P), 0.0, ALU.add, ALU.max))
            dve.reduce_sum(used_c, mine, axis=AX.X)
            for col, of_list in ((start_c, starts), (over_c, counts), (base_c, base0), (weight_c, iota_l), (list_c, w_start)):
                step(dve.tensor_tensor(t5, mine, of_list, ALU.mult))
                step(dve.reduce_sum(col, t5, axis=AX.X))
            shared(7)
            step(dve.tensor_tensor(dup_c, pcol, start_c, ALU.subtract))
            step(dve.tensor_scalar(dup_c, dup_c, float(P), None, ALU.mult))
            step(dve.tensor_tensor(row_c, dup_c, over_c, ALU.min))
            step(dve.tensor_tensor(dup_c, dup_c, row_c, ALU.subtract))
            step(dve.tensor_tensor(row_c, row_c, base_c, ALU.add))
            step(dve.tensor_scalar(used_c, used_c, -float(DUMMY_ROW), float(DUMMY_ROW), ALU.mult, ALU.add))
            dve.tensor_tensor(row_c, row_c, used_c, ALU.add)
            dve.tensor_scalar(dups[:, :], ident[:, :], dup_c, None, ALU.mult)
            dve.tensor_scalar(weight_c, weight_c, float(D), None, ALU.add).then_inc(cols_ok, 1)

            for t in range(8, NT):
                shared(t)
                if t == TABLE_AFTER + 1:
                    dve.wait_ge(table_ps, 1)
                    dve.tensor_copy(table[:, :, :].rearrange("p a b -> p (a b)"), B[6][0:1, 0:3 * P])
                    dve.tensor_scalar(fresh[:, :], B[6][:, 3 * P:4 * P], pcol, None, ALU.is_le).then_inc(table_ok, 1)
                    dve.wait_ge(table_ok, 1)
            s_add(NT - 2)
            s_add(NT - 1)

            def take_rows(i, v):
                dyn = not isinstance(i, int)
                dve.wait_ge(T_ps, i + 1)
                if dyn or i >= 2:
                    dve.wait_ge(U_ps, i - 1)
                dve.tensor_copy(GT[:, v % 2, :, :].rearrange("p k s -> p (k s)"), B[v % 2][:, 0:D]).then_inc(gt_ok, 1)
                at = entry(mybir.EngineType.DVE, 2, i, ROW - 1)
                dve.tensor_tensor(wcol[:, bass.ds(i, 1)], G[:, v % 4, bass.ds(at, 1)], fresh[:, bass.ds(i, 1)], ALU.mult)
                dve.tensor_copy(tok_of[:, bass.ds(i, 1)], G_i[:, v % 4, ROW - 1:ROW]).then_inc(meta_ok, 1)

            def hidden(i, u, anchor):
                dve.wait_ge(silu_ok, i + 1)
                if anchor:
                    if isinstance(i, int) and i < ROUTED_TILES + 2:
                        dve.memset(H[ANCHOR_HIDDEN:P, u % 2, :], 0.0)
                    n = ANCHOR_HIDDEN
                    ups = B[2 + u % 2][n:2 * n, 0:P]
                else:
                    n = HIDDEN
                    ups = B[2 + u % 2][:, P:2 * P]
                dve.tensor_tensor(H[0:n, u % 2, :], S[0:n, u % 2, :], ups, ALU.mult).then_inc(H_ok, 1)
                if not isinstance(i, int) or i + 2 < XT:
                    take_rows(i + 2, u + 2)

            take_rows(0, 0)
            take_rows(1, 1)
            groups(dve, hidden)
            def add_sums(q, c):
                lo, hi = PIECES[q]
                return dve.tensor_tensor(h[0:TP, lo:hi, :], h[0:TP, lo:hi, :], sums[:, c, lo:hi, :], ALU.add)

            for q in range(len(PIECES)):
                dve.wait_ge(fin_ld[q][0], 16 * 2)
                step(add_sums(q, 0))
                step(add_sums(q, 1))
                dve.wait_ge(fin_pair, q + 1)
                add_sums(q, 2).then_inc(fin_ok, 1)


def host_layout(a):
    f = {k: np.asarray(v) for k, v in a.items()}

    def chunks(m):
        return m.reshape(-1, P, m.shape[-1]).transpose(1, 0, 2)

    x = f["x"].reshape(IMAGES, 3, 6, 16, 6, 16).transpose(1, 3, 5, 0, 2, 4).reshape(PC * P, IMAGES, PATCHES)
    patches = np.zeros((PC * P, IMAGES, SEQ), x.dtype)
    patches[:, :, 1:] = x
    pos = np.concatenate([f["cls_tok"][0], f["L0_tok_pos_embd"][0]], 0)
    bias = np.zeros((SEQ, D), pos.dtype)
    bias[1:] = f["L0_tok_b"]
    wq, wk, wv = f["L0_attn_Wq"], f["L0_attn_Wk"], f["L0_attn_Wv"]

    def lists(gate, up, down):
        n, _, hidden = gate.shape
        both = np.stack([m.reshape(n, KC, P, hidden).transpose(2, 0, 1, 3) for m in (gate, up)], 3)
        w = np.zeros((P, n, 2 * KC * hidden + D), gate.dtype)
        w[:, :, 0:2 * KC * hidden] = both.reshape(P, n, 2 * KC * hidden)
        w[0:hidden, :, 2 * KC * hidden:] = down.transpose(1, 0, 2)
        return w.reshape(P, -1)

    wx = np.concatenate([lists(f["L0_ffn_w_gate"], f["L0_ffn_w_up"], f["L0_ffn_w_down"]),
                         lists(f["L0_ffn_anchor_w_gate"], f["L0_ffn_anchor_w_up"], f["L0_ffn_anchor_w_down"])], 1)
    return dict(
        pt=chunks(patches.reshape(PC * P, TOKENS)), wt=chunks(f["L0_tok_W"].T),
        posr=np.tile(pos, (3, 1)), brow=np.tile(bias, (3, 1)),
        wqkv=chunks(np.concatenate([wq, wk, wv], 1)), wo=chunks(f["L0_attn_Wo"]), wg1=chunks(f["L0_attn_Wg1"]),
        wg2=f["L0_attn_Wg2"], lnwb=chunks(np.stack([f["L0_attn_ln_w"], f["L0_attn_ln_b"]], 1)),
        gwt=chunks(f["L0_ffn_gate_weight"].T), gbias=np.tile(f["L0_ffn_gate_bias"], (P, 1)),
        sgu=chunks(np.concatenate([f["L0_ffn_shared_w_gate"], f["L0_ffn_shared_w_up"]], 1)),
        sd=f["L0_ffn_shared_w_down"], wx=wx)


def constants():
    tok = np.arange(TT)
    img, pos = tok // SEQ, tok % SEQ
    causal = ((img[:, None] == img[None]) & (pos[None] >= pos[:, None])).astype(np.float32)
    hmask = (np.arange(P)[:, None] // HD == np.arange(HEADS // KC)[None]).astype(np.float32)
    inv = (1.0 / np.float32(10000.0) ** (np.arange(0, HD, 2, dtype=np.float32) / np.float32(HD))).astype(np.float32)
    ang = pos.astype(np.float32)[:, None] * inv[None]
    cos, sin = np.cos(ang), np.sin(ang)
    cs = np.stack([np.concatenate([cos, cos], 1), np.concatenate([-sin, sin], 1)], 1)
    before = np.triu(np.ones((P, P), np.float32), 1)
    small = np.zeros((P, 3 * LISTS + 16 + 2), np.float32)
    small[:, 0:LISTS] = np.arange(LISTS)
    small[:, LISTS:2 * LISTS] = np.arange(LISTS) * LIST_ROWS
    small[:, 2 * LISTS:2 * LISTS + 16] = np.tril(np.ones((GROUPS, GROUPS)), -1).ravel()
    small[:, 2 * LISTS + 16] = np.arange(P)
    small[:, 2 * LISTS + 17:3 * LISTS + 17] = [e * WX if e < EXPERTS else EXPERTS * WX + (e - EXPERTS) * ANCHOR_WX
                                               for e in range(LISTS)]
    return dict(ident_c=np.eye(P, dtype=np.float32), cmask_c=causal, hmask_c=hmask, cs_c=cs.astype(np.float32),
                before_c=before, small_c=small)


def kernel(**inputs):
    import concourse.bacc as bacc
    from concourse.bass_utils import run_bass_kernel_spmd

    nc = bacc.Bacc("TRN2", target_bir_lowering=False, num_devices=1)
    arrays, args = {}, {}
    for name, a in {**host_layout(inputs), **constants()}.items():
        a = np.ascontiguousarray(a)
        arrays[f"in_{name}"] = a
        args[name] = nc.dram_tensor(f"in_{name}", a.shape, mybir.dt.from_np(a.dtype), kind="ExternalInput").ap()
    out = nc.dram_tensor("out_h", (FILL_ROW, D), F32, kind="ExternalOutput").ap()
    build(nc, **args, out=out)
    r = run_bass_kernel_spmd(nc, [arrays], core_ids=[0])
    rows = r.results[0]["out_h"].reshape(NT, TP, D)[:, :TT].reshape(NT * TT, D)
    return rows[:TOKENS].reshape(IMAGES, SEQ, D)
```
